# Optimizing a Trainium2 kernel written in Bass

```python
import numpy as np
import jax
import jax.numpy as jnp

def _softmax(x, axis=-1):
    return jax.nn.softmax(x, axis=axis)

def _gelu(x):
    return jax.nn.gelu(x, approximate=True)

def _silu(x):
    return jax.nn.silu(x)

def _sigmoid(x):
    return jax.nn.sigmoid(x)

def _layernorm(x, axis=-1, eps=1e-05):
    m = jnp.mean(x, axis=axis, keepdims=True)
    v = jnp.var(x, axis=axis, keepdims=True)
    return (x - m) / jnp.sqrt(v + eps)

def _scatter_add(tgt, idx, src, axis=0):
    return tgt.at[idx].add(src)

def _segment_sum(src, seg, n):
    return jax.ops.segment_sum(src, seg, n)
kernel_name = 'mk_gps_d1_gnn_r8_b81417'

def setup_inputs(seed: int=0):
    np.random.seed(seed)
    _w = jnp.asarray

    def _rec_inputs():
        import jax
        import jax.numpy as jnp
        _gk = jax.random.key(seed)
        x = -0.0002117 + 1 * jax.random.normal(jax.random.fold_in(_gk, 1), (6250, 256), jnp.float32)
        _s = jax.random.randint(jax.random.fold_in(_gk, 2), (100000,), 0, 6250, jnp.int32)
        _d = jax.random.randint(jax.random.fold_in(_gk, 3), (100000,), 0, 6250, jnp.int32)
        _loop = jnp.arange(6250, dtype=jnp.int32)
        src = jnp.concatenate([_s, _d, _loop])
        dst = jnp.concatenate([_d, _s, _loop])
        _o = jnp.argsort(dst, stable=True)
        src = src[_o]
        dst = dst[_o]
        edge_weight = jax.random.uniform(jax.random.fold_in(_gk, 12), (206250,), jnp.float32, 0.0, 1)
        return (x, src, dst, edge_weight)
    x, src, dst, edge_weight = _rec_inputs()

    def _L0_gnn_setup():
        import jax, jax.numpy as jnp
        import numpy as np
        N = 12500
        E = 400000
        F_IN = 256
        F_OUT = 256

        def _spmm(edge_index, edge_weight, x, n):
            dst, src = (edge_index[0], edge_index[1])
            msg = edge_weight[:, None] * x[src]
            return jax.ops.segment_sum(msg, dst, num_segments=n)
        key = jax.random.key(seed)
        k1, k2, k3, k4, k5 = jax.random.split(key, 5)
        feature = jax.random.normal(k1, (N, F_IN), dtype=jnp.float32)
        edge_index = jax.random.randint(k2, (2, E), 0, N)
        edge_weight = jax.random.uniform(k3, (E,), dtype=jnp.float32)
        stdv = 1.0 / np.sqrt(F_OUT)
        weight = jax.random.uniform(k4, (F_IN, F_OUT), dtype=jnp.float32, minval=-stdv, maxval=stdv)
        bias = jax.random.uniform(k5, (F_OUT,), dtype=jnp.float32, minval=-stdv, maxval=stdv)
        return {'feature': feature, 'edge_weight': edge_weight, 'weight': weight, 'bias': bias, 'edge_index': edge_index, 'mode': 2}
    _L0_gnn_all = _L0_gnn_setup()
    _L0_gnn_in = {k: v for k, v in _L0_gnn_all.items() if k in ('weight', 'bias')}
    del _L0_gnn_all

    def _L0_mix_setup():
        import jax, jax.numpy as jnp
        import numpy as np
        HEADS, DIM_HEAD = (8, 64)
        EPS = 1e-05

        def instance_norm(t):
            mu = jnp.mean(t, axis=-1, keepdims=True)
            var = jnp.mean((t - mu) ** 2, axis=-1, keepdims=True)
            return (t - mu) * jax.lax.rsqrt(var + EPS)
        key = jax.random.key(seed)
        k1, k2, k3, k4 = jax.random.split(key, 4)
        B, N, D = (8, 1024, 256)
        inner = HEADS * DIM_HEAD
        x = jax.random.normal(k1, (B, N, D), jnp.float32)
        w_qkv = jax.random.normal(k2, (3 * inner, D), jnp.float32) / np.sqrt(D).astype(np.float32)
        w_out = jax.random.normal(k3, (D, inner), jnp.float32) / np.sqrt(inner).astype(np.float32)
        b_out = 0.01 * jax.random.normal(k4, (D,), jnp.float32)
        return {'x': x, 'w_qkv': w_qkv, 'w_out': w_out, 'b_out': b_out}
    _L0_mix_all = _L0_mix_setup()
    _L0_mix_in = {k: v for k, v in _L0_mix_all.items() if k in ('w_qkv', 'w_out', 'b_out')}
    del _L0_mix_all

    def _L0_ffn_setup():
        import jax, jax.numpy as jnp
        import numpy as np
        NUM_EXPERTS = 8
        TOP_K = 2
        B, S, D = (8, 1024, 256)

        def _moe(tokens, router_w, w1, b1, w2, b2):
            N = tokens.shape[0]
            E = router_w.shape[0]
            logits = tokens.astype(jnp.float32) @ router_w.astype(jnp.float32).T
            probs = jax.nn.softmax(logits, axis=-1)
            rw, re = jax.lax.top_k(probs, TOP_K)
            if TOP_K > 1:
                rw = rw / jnp.maximum(rw.sum(-1, keepdims=True), 1e-12)
            rw = rw.astype(tokens.dtype)
            combine = jnp.zeros((N, E), tokens.dtype).at[jnp.arange(N)[:, None], re].set(rw)
            out = tokens
            for e in range(E):
                h = jax.nn.gelu(tokens @ w1[e] + b1[e], approximate=False)
                y = h @ w2[e] + b2[e]
                out = out + combine[:, e:e + 1] * y
            return out
        key = jax.random.key(seed)
        ks = jax.random.split(key, 4)
        scale = 1.0 / np.sqrt(D).astype(np.float32)
        return {'input_embeddings': jax.random.normal(ks[0], (B, S, D), jnp.float32), 'router_w': jax.random.normal(ks[1], (NUM_EXPERTS, D), jnp.float32) * scale, 'w1': jax.random.normal(ks[2], (NUM_EXPERTS, D, D), jnp.float32) * scale, 'b1': jnp.zeros((NUM_EXPERTS, D), jnp.float32), 'w2': jax.random.normal(ks[3], (NUM_EXPERTS, D, D), jnp.float32) * scale, 'b2': jnp.zeros((NUM_EXPERTS, D), jnp.float32)}
    _L0_ffn_all = _L0_ffn_setup()
    _L0_ffn_in = {k: v for k, v in _L0_ffn_all.items() if k in ('router_w', 'w1', 'b1', 'w2', 'b2')}
    del _L0_ffn_all
    return {'x': x, 'src': src, 'dst': dst, 'edge_weight': edge_weight, 'L0_gnn_weight': _L0_gnn_in['weight'], 'L0_gnn_bias': _L0_gnn_in['bias'], 'L0_mix_w_qkv': _L0_mix_in['w_qkv'], 'L0_mix_w_out': _L0_mix_in['w_out'], 'L0_mix_b_out': _L0_mix_in['b_out'], 'L0_ffn_router_w': _L0_ffn_in['router_w'], 'L0_ffn_w1': _L0_ffn_in['w1'], 'L0_ffn_b1': _L0_ffn_in['b1'], 'L0_ffn_w2': _L0_ffn_in['w2'], 'L0_ffn_b2': _L0_ffn_in['b2']}

def reference(x, src, dst, edge_weight, L0_gnn_weight, L0_gnn_bias, L0_mix_w_qkv, L0_mix_w_out, L0_mix_b_out, L0_ffn_router_w, L0_ffn_w1, L0_ffn_b1, L0_ffn_w2, L0_ffn_b2):
    import jax
    import jax.numpy as jnp

    def _L0_gnn_ref(feature, edge_weight, weight, bias, edge_index, mode):
        import jax, jax.numpy as jnp
        import numpy as np
        N = 12500
        E = 400000
        F_IN = 256
        F_OUT = 256

        def _spmm(edge_index, edge_weight, x, n):
            dst, src = (edge_index[0], edge_index[1])
            msg = edge_weight[:, None] * x[src]
            return jax.ops.segment_sum(msg, dst, num_segments=n)
        if mode in (1, 2):
            feature = feature - jnp.mean(feature, axis=0, keepdims=True)
        if mode == 2:
            std = jnp.std(feature, axis=0, ddof=1) + 0.0001
            feature = feature / std
        support = _spmm(edge_index, edge_weight, feature, feature.shape[0])
        output = support @ weight
        return output + bias

    def _L0_mix_ref(x, w_qkv, w_out, b_out):
        import jax, jax.numpy as jnp
        import numpy as np
        HEADS, DIM_HEAD = (8, 64)
        EPS = 1e-05

        def instance_norm(t):
            mu = jnp.mean(t, axis=-1, keepdims=True)
            var = jnp.mean((t - mu) ** 2, axis=-1, keepdims=True)
            return (t - mu) * jax.lax.rsqrt(var + EPS)
        B, N, _ = x.shape
        H, Dh = (HEADS, DIM_HEAD)
        qkv = jnp.einsum('bnd,ed->bne', x, w_qkv)
        q, k, v = jnp.split(qkv, 3, axis=-1)

        def to_heads(t):
            return t.reshape(B, N, H, Dh).transpose(0, 2, 1, 3)
        q, k, v = (to_heads(q), to_heads(k), to_heads(v))
        k = instance_norm(k)
        v = instance_norm(v)
        dots = jnp.einsum('bhnd,bhne->bhde', k, v)
        out = jnp.einsum('bhnd,bhde->bhne', q, dots) / N
        out = out.transpose(0, 2, 1, 3).reshape(B, N, H * Dh)
        return jnp.einsum('bne,de->bnd', out, w_out) + b_out

    def _L0_ffn_ref(input_embeddings, router_w, w1, b1, w2, b2):
        import jax, jax.numpy as jnp
        import numpy as np
        NUM_EXPERTS = 8
        TOP_K = 2
        B, S, D = (8, 1024, 256)

        def _moe(tokens, router_w, w1, b1, w2, b2):
            N = tokens.shape[0]
            E = router_w.shape[0]
            logits = tokens.astype(jnp.float32) @ router_w.astype(jnp.float32).T
            probs = jax.nn.softmax(logits, axis=-1)
            rw, re = jax.lax.top_k(probs, TOP_K)
            if TOP_K > 1:
                rw = rw / jnp.maximum(rw.sum(-1, keepdims=True), 1e-12)
            rw = rw.astype(tokens.dtype)
            combine = jnp.zeros((N, E), tokens.dtype).at[jnp.arange(N)[:, None], re].set(rw)
            out = tokens
            for e in range(E):
                h = jax.nn.gelu(tokens @ w1[e] + b1[e], approximate=False)
                y = h @ w2[e] + b2[e]
                out = out + combine[:, e:e + 1] * y
            return out
        b, s, d = input_embeddings.shape
        tokens = input_embeddings.reshape(b * s, d)
        return _moe(tokens, router_w, w1, b1, w2, b2).reshape(b, s, d)
    edge_index = jnp.stack([src, dst])
    xn = _layernorm(x, axis=-1)
    x = x + _L0_gnn_ref(xn, edge_weight, L0_gnn_weight, L0_gnn_bias, edge_index, 2) + _L0_mix_ref(xn[None], L0_mix_w_qkv, L0_mix_w_out, L0_mix_b_out)[0]
    x = x + _L0_ffn_ref(_layernorm(x, axis=-1)[None], L0_ffn_router_w, L0_ffn_w1, L0_ffn_b1, L0_ffn_w2, L0_ffn_b2)[0]
    return x

_drawn_inputs = setup_inputs


def setup_inputs(seed=0):
    import zlib

    import numpy as np

    out = dict(_drawn_inputs(seed))
    spreads = {'L0_ffn_b1': (0.0, 0.514), 'L0_ffn_b2': (0.0, 0.349)}
    factors = {'L0_mix_b_out': 7.128}
    for name, (base, spread) in spreads.items():
        noise = np.random.default_rng([zlib.crc32(name.encode()), seed]).standard_normal(out[name].shape)
        drawn = base * np.exp(spread * noise) if base else spread * noise
        out[name] = jnp.asarray(drawn.astype(out[name].dtype))
    for name, factor in factors.items():
        out[name] = (out[name] * factor).astype(out[name].dtype)
    return out
```

```python
import concourse.bass as bass
from concourse import mybir
from contextlib import ExitStack

F32 = mybir.dt.float32
I32 = mybir.dt.int32
ALU = mybir.AluOpType
ACT = mybir.ActivationFunctionType
AX = mybir.AxisListType

P = 128
N = 6250
D = 256
KD = D // P
TILES = -(-N // P)
FULL = N // P
LAST = N - FULL * P
NPAD = TILES * P
EDGES = 206250
EPT = 8
QT = 4
GE = EPT * P
GROUPS = -(-EDGES // GE)
REPEATED = GROUPS * GE - EDGES
COLS = GROUPS * EPT
QUADS = COLS // QT
SUMS = QT
ROWS = TILES * P + P
HEADS, DH = 8, 64
INNER = HEADS * DH
PAIRS = HEADS // 2
EXPERTS = 8
EPS = 1e-5
GB = GROUPS // 2
CH = 250
CHUNKS = N // CH


class Chain:

    def __init__(self, eng, sem, base=0):
        self.eng, self.sem, self.base, self.n = eng, sem, base, 0

    def __call__(self, ins):
        self.n += 1
        ins.then_inc(self.sem, 1)
        self.eng.wait_ge(self.sem, self.base + self.n)


def over_tiles(eng, count, unroll, body):
    rounds = count // unroll
    with eng.Fori(0, rounds) as i:
        for u in range(unroll):
            body(i * unroll + u, u)
    for t in range(rounds * unroll, count):
        body(t, t % unroll)


def build(nc, x, src, dst, ew, src_rows, w_gnn, b_gnn, w_kvT, w_q, w_outT, b_out,
          w_routerT, w1, b1T, w2, b2, out):
    ctx = ExitStack()
    with ctx:
        def sb(name, shape, dt=F32):
            return ctx.enter_context(nc.sbuf_tensor(name, shape, dt))

        def ps(name, shape):
            return ctx.enter_context(nc.psum_tensor(name, shape, F32))

        def sem(name):
            return ctx.enter_context(nc.semaphore(name))

        feat_rows = nc.dram_tensor("feat_rows", (ROWS, D), F32).ap()
        edge_sums = [nc.dram_tensor(f"edge_sums{r}", (ROWS, D), F32).ap() for r in range(SUMS)]

        acc = sb("acc", [P, TILES, D])
        xnT = sb("xnT", [P, KD, NPAD])
        edge_area = sb("edge_area", [P, 3 * COLS + 4 * QT * D])
        src_tab = edge_area[:, 0:COLS]
        dst_tab = edge_area[:, COLS:2 * COLS]
        ew_tab = edge_area[:, 2 * COLS:3 * COLS]
        msg = edge_area[:, 3 * COLS:].rearrange("p (s j d) -> p s j d", s=4, j=QT)
        raw = [edge_area[:, (3 + i) * COLS:(4 + i) * COLS].bitcast(I32) for i in range(2)]
        w1_sb = edge_area[:, 0:EXPERTS * KD * D].rearrange("p (e k n) -> p e k n", e=EXPERTS, k=KD)
        w2_sb = edge_area[:, EXPERTS * KD * D:2 * EXPERTS * KD * D].rearrange("p (e k n) -> p e k n", e=EXPERTS, k=KD)
        src_row = sb("src_row", [P, 2, QT, P], I32)
        same = sb("same", [P, 2, QT, P])
        onehot = sb("onehot", [P, 2, QT, P])
        joined = sb("joined", [P, 2, QT, P])
        window = sb("window", [P, 2, D])
        rest_onehot = sb("rest_onehot", [P, QT, P])
        rest_joined = sb("rest_joined", [P, P])
        rest_window = sb("rest_window", [P, D])
        earlier = sb("earlier", [P, P])
        spare = sb("spare", [P, 1])
        unused = sb("unused", [P, QT, P], mybir.dt.bfloat16)
        clash = sb("clash", [P, 4, 3, QT])
        target = sb("target", [P, 4, QT], I32)
        wkv = sb("wkv", [P, KD, 2 * INNER])
        wq = sb("wq", [P, PAIRS, D])
        woT = sb("woT", [P, PAIRS, D])
        wg = sb("wg", [P, KD, D])
        wr = sb("wr", [P, KD, EXPERTS])
        b1_sb = sb("b1_sb", [P, EXPERTS, KD])
        b2_sb = sb("b2_sb", [EXPERTS, D])
        ident = sb("ident", [P, P])
        iota = sb("iota", [P, P])
        ones = sb("ones", [P, P])
        eps = sb("eps", [P, 1])
        zeros = sb("zeros", [P, D])
        brow = sb("brow", [1, 3, D])
        work = sb("work", [P, 2, D])
        ring = sb("ring", [P, 2, KD, P])
        sq = sb("sq", [P, 2, HEADS, DH])
        k_sb = sb("k_sb", [P, INNER])
        v_sb = sb("v_sb", [P, HEADS, DH])
        hs = sb("hs", [P, 3, 2 * HEADS])
        stats = sb("stats", [P, 2 * CHUNKS, 6])
        ln = sb("ln", [P, 6, TILES])
        fm = sb("fm", [P, KD, 4])
        bounds = sb("bounds", [P, 2, GROUPS])
        bcol = sb("bcol", [GB, 2, 2])
        bcol_i = sb("bcol_i", [GB, 2, 1], I32)
        upper = sb("upper", [GB, 2, GROUPS])
        table = sb("table", [1, 3, GROUPS], I32)
        dots_sb = sb("dots_sb", [P, PAIRS, P])
        pq_sb = sq[:, :, :, :].rearrange("p a h c -> p (a h c)").rearrange("p (q d) -> p q d", q=PAIRS)
        mix = sb("mix", [P, KD, D])
        tiny = sb("tiny", [1, 4])
        router = wkv[:, :, :].rearrange("p k n -> p (k n)")[:, 0:5 * TILES * EXPERTS].rearrange(
            "p (a t e) -> p a t e", a=5, t=TILES)
        route1 = sb("route1", [P, 4, TILES])
        rank = sb("rank", [P, EXPERTS])
        combT = sb("combT", [EXPERTS, P])
        comb1 = sb("comb1", [P, EXPERTS])

        bank = [ps(f"bank{i}", [P, 512]) for i in range(8)]

        s_x = [sem(f"x_loaded{i}") for i in range(5)]
        s_w = sem("weights_loaded")
        s_dst = sem("dst_loaded")
        s_pad = sem("pad_cleared")
        s_const = sem("constants_made")
        s_zero = sem("sums_cleared")
        LOADS = 10
        s_ch = sem("a_vector_chain")
        s_pch = sem("a_pool_chain")
        s_var = sem("a_variance_ready")
        s_std = sem("a_deviation_ready")
        s_row = sem("a_row_ready")
        s_turn = sem("a_row_turned")
        s_kept = sem("a_row_kept")
        XC = 12
        with nc.Block() as block:
            @block.sync
            def _(sp):
                for c in range(FULL // XC):
                    sp.dma_start(acc[:, c * XC:(c + 1) * XC, :],
                                 x[c * XC * P:(c + 1) * XC * P, :].rearrange("(t p) d -> p t d", p=P)).then_inc(s_x[c], 16)
                sp.wait_ge(s_pad, 1)
                sp.dma_start(acc[0:LAST, FULL, :], x[FULL * P:N, :]).then_inc(s_x[4], 16)
                sp.dma_start(raw[0], dst).then_inc(s_dst, 16)
                sp.dma_start(raw[1], src).then_inc(s_dst, 16)
                n = 0
                for to, of in ((wkv[:, :, :], w_kvT.rearrange("(k p) e -> p k e", p=P)),
                               (ew_tab, ew),
                               (wg[:, :, :], w_gnn.rearrange("(k p) e -> p k e", p=P)),
                               (wq[:, :, :], w_q.rearrange("(k p) e -> p k e", p=P)),
                               (woT[:, :, :], w_outT.rearrange("(k p) e -> p k e", p=P)),
                               (wr[:, :, :], w_routerT.rearrange("(k p) e -> p k e", p=P)),
                               (b1_sb[:, :, :], b1T),
                               (b2_sb[:, :], b2),
                               (brow[:, 0, :], b_gnn), (brow[:, 1, :], b_out)):
                    sp.dma_start(to, of).then_inc(s_w, 16)
                    n += 16
                assert n == 16 * LOADS
                sp.wait_ge(s_pad, 2)
                for to in edge_sums:
                    sp.dma_start(to.rearrange("(t p) d -> p t d", p=P),
                                 zeros[:, :].unsqueeze(1).to_broadcast([P, ROWS // P, D])).then_inc(s_zero, 16)
                sp.dma_start(feat_rows[NPAD:ROWS, :], zeros[:, :]).then_inc(s_zero, 16)
                sp.wait_ge(s_w, n)
                sp.wait_ge(s_dst, 32)
                sp.wait_ge(s_zero, 16 * (SUMS + 1))

            @block.gpsimd
            def _(pool):
                link = Chain(pool, s_pch)
                link(nc.gpsimd.memset(ident[:, :], 0.0))
                nc.gpsimd.affine_select(out=ident[:, :], in_=ident[:, :], compare_op=ALU.not_equal, fill=1.0, base=0,
                                        pattern=[[-1, P]], channel_multiplier=1).then_inc(s_const, 1)
                nc.gpsimd.iota(iota[:, :], pattern=[[1, P]], base=0, channel_multiplier=0,
                               allow_small_or_imprecise_dtypes=True).then_inc(s_const, 1)
                nc.gpsimd.iota(rank[:, :], pattern=[[-1, EXPERTS]], base=EXPERTS, channel_multiplier=0,
                               allow_small_or_imprecise_dtypes=True).then_inc(s_const, 1)
                for b in range(2):
                    link(nc.gpsimd.memset(upper[:, b, :], 1.0))
                    nc.gpsimd.affine_select(out=upper[:, b, :], in_=upper[:, b, :], compare_op=ALU.is_gt, fill=0.0,
                                            base=-b * GB, pattern=[[1, GROUPS]], channel_multiplier=-1).then_inc(s_const, 1)
                pool.wait_ge(s_w, 16 * LOADS)
                tail = ew_tab[:, COLS - EPT:COLS]
                nc.gpsimd.affine_select(out=tail, in_=tail, compare_op=ALU.is_ge, fill=0.0, base=-REPEATED,
                                        pattern=[[P, EPT]], channel_multiplier=1).then_inc(s_const, 1)
                link(nc.gpsimd.memset(earlier[:, :], 1.0))
                nc.gpsimd.affine_select(out=earlier[:, :], in_=earlier[:, :], compare_op=ALU.is_gt, fill=0.0, base=0,
                                        pattern=[[-1, P]], channel_multiplier=1).then_inc(s_const, 1)
                nc.gpsimd.iota(spare[:, :], pattern=[[0, 1]], base=N, channel_multiplier=1,
                               allow_small_or_imprecise_dtypes=True).then_inc(s_const, 1)

            @block.vector
            def _(dve):
                nc.vector.memset(acc[:, FULL, :], 0.0).then_inc(s_pad, 1)
                link = Chain(dve, s_ch)
                nc.vector.memset(eps[:, :], EPS)
                nc.vector.memset(ones[:, :], 1.0)
                nc.vector.memset(zeros[:, :], 0.0).then_inc(s_pad, 1)
                link(nc.vector.memset(dots_sb[:, :, :], 0.0))
                for c in range(FULL // XC):
                    dve.wait_ge(s_x[c], 16)
                    for t in range(c * XC, (c + 1) * XC):
                        nc.vector.bn_stats(stats[:, t % (2 * CHUNKS), :], acc[:, t, :])
                dve.wait_ge(s_x[4], 16)
                link(nc.vector.bn_stats(stats[:, FULL, :], acc[:, FULL, :]))
                row_statistics(link, nc, stats, ln, s_var)
                dve.wait_ge(s_std, 1)
                link(nc.vector.reciprocal(ln[:, 1, :], ln[:, 2, :]))
                base = link.n

                def row(t, slot):
                    dve.wait_ge(s_turn, t + 1)
                    nc.vector.tensor_scalar(work[:, slot, :], acc[:, bass.ds(t, 1), :], ln[:, 0, bass.ds(t, 1)],
                                            ln[:, 1, bass.ds(t, 1)], ALU.subtract, ALU.mult).then_inc(s_row, 1)
                over_tiles(dve, TILES, 2, row)

                for k in range(KD):
                    dve.wait_ge(s_kept, TILES + 2)
                    for c in range(CHUNKS):
                        last = nc.vector.bn_stats(stats[:, c, :], xnT[:, k, c * CH:(c + 1) * CH])
                    link(last)
                    link(nc.vector.bn_aggr(fm[:, k, 0:2], stats[:, 0:CHUNKS, :].rearrange("p c s -> p (c s)")))
                nc.vector.tensor_copy(fm[:, 0, 2:3], fm[:, 0, 1:2]).then_inc(s_var, 1)
                dve.wait_ge(s_std, 3)
                for k in range(KD):
                    link(nc.vector.tensor_scalar_add(fm[:, k, 2:3], fm[:, k, 3:4], 1e-4))
                    link(nc.vector.reciprocal(fm[:, k, 3:4], fm[:, k, 2:3]))

                dve.wait_ge(s_w, 16 * LOADS)
                heads = wkv[:, :, :].rearrange("p k (h c) -> p (k h) c", c=DH)
                hm = sq[:, 0, 0, 0:2 * 2 * HEADS]
                link(nc.vector.tensor_reduce(hm, heads, AX.X, ALU.add))
                link(nc.vector.tensor_scalar_mul(hm, hm, 1.0 / DH))
                link(nc.vector.tensor_tensor(heads, heads, hm.unsqueeze(2).to_broadcast([P, 4 * HEADS, DH]), ALU.subtract))
                link(nc.vector.tensor_tensor(brow[:, 2, :], brow[:, 0, :], brow[:, 1, :], ALU.add))

                dve.wait_ge(s_dst, 32)
                nc.vector.tensor_copy(src_tab, raw[1])
                link(nc.vector.tensor_copy(dst_tab, raw[0]))
                by_group = dst_tab.rearrange("p (g j) -> p g j", j=EPT)
                nc.vector.tensor_reduce(bounds[:, 0, :], by_group, AX.X, ALU.min)
                nc.vector.tensor_reduce(bounds[:, 1, :], by_group, AX.X, ALU.max).then_inc(s_var, 1)

            @block.scalar
            def _(act):
                act.wait_ge(s_var, 1)
                nc.scalar.activation(ln[:, 2, :], ln[:, 1, :], ACT.Sqrt, bias=eps[:, :]).then_inc(s_std, 1)

                def keep(t, slot):
                    act.wait_ge(s_turn, t + 3)
                    to = xnT[:, :, bass.ds(t * P, P)]
                    nc.scalar.copy(to, bank[slot][:, 0:D].rearrange("p (k n) -> p k n", k=KD)).then_inc(s_kept, 1)
                act.sem_inc(s_kept, 2)
                over_tiles(act, TILES, 2, keep)
                act.wait_ge(s_var, 2)
                for k in range(KD):
                    nc.scalar.activation(fm[:, k, 3:4], fm[:, k, 1:2], ACT.Sqrt, scale=N / (N - 1.0)).then_inc(s_std, 1)

            @block.tensor
            def _(pe):
                pe.wait_ge(s_const, 1)
                pe.sem_inc(s_turn, 2)

                def turn(t, slot):
                    pe.wait_ge(s_row, t + 1)
                    pe.wait_ge(s_kept, t + 1)
                    for k in range(KD):
                        last = nc.tensor.transpose(bank[slot][:, k * P:(k + 1) * P], work[:, slot, k * P:(k + 1) * P], ident[:, :])
                    last.then_inc(s_turn, 1)
                over_tiles(pe, TILES, 2, turn)

        b_ready = sem("b_operand_ready")
        b_done = sem("b_product_ready")
        b_copied = sem("b_product_copied")
        b_stored = [sem(f"b_rows_stored{i}") for i in range(2)]
        b_ch = sem("b_vector_chain")
        b_bt = sem("b_bounds_turned")
        b_bc = sem("b_bounds_columns")
        b_br = sem("b_bounds_rows")
        with nc.Block() as block:
            @block.vector
            def _(dve):
                def operand(t, slot):
                    dve.wait_ge(b_done, t + 1)
                    for k in range(KD):
                        last = nc.vector.tensor_scalar(ring[:, slot, k, :], xnT[:, k, bass.ds(t * P, P)], fm[:, k, 0:1],
                                                       fm[:, k, 3:4], ALU.subtract, ALU.mult)
                    last.then_inc(b_ready, 1)
                over_tiles(dve, TILES, 2, operand)

                link = Chain(dve, b_ch)
                dve.wait_ge(b_bt, 1)
                for b in range(2):
                    for m, op in ((0, ALU.min), (1, ALU.max)):
                        link(nc.vector.tensor_reduce(bcol[:, b, m:m + 1], bank[2 + b][0:GB, m * P:(m + 1) * P], AX.X, op))
                link(nc.vector.tensor_tensor(bcol_i[:, :, :], bcol[:, :, 1:2], bcol[:, :, 0:1], ALU.subtract))
                link(nc.vector.tensor_single_scalar(bcol_i[:, :, :], bcol_i[:, :, :], 7, ALU.arith_shift_right))
                nc.vector.tensor_copy(bcol[:, :, 1:2], bcol_i[:, :, :]).then_inc(b_bc, 1)
                dve.wait_ge(b_br, 1)
                nc.vector.tensor_copy(table[:, 0, :], bank[4][0:1, 0:GROUPS])
                nc.vector.tensor_copy(table[:, 1, :], bank[4][0:1, 256:256 + GROUPS])
                nc.vector.tensor_scalar_mul(table[:, 2, :], bank[5][0:1, 0:GROUPS], 2.0)
                by_group = dst_tab.rearrange("p (g j) -> p g j", j=EPT)
                link(nc.vector.tensor_tensor(by_group, by_group, bank[6][:, 0:GROUPS].unsqueeze(2).to_broadcast([P, GROUPS, EPT]),
                                             ALU.subtract))

            @block.tensor
            def _(pe):
                pe.sem_inc(b_done, 2)

                def product(t, slot):
                    pe.wait_ge(b_ready, t + 1)
                    pe.wait_ge(b_copied, t + 1)
                    for k in range(KD):
                        last = nc.tensor.matmul(bank[slot][:, 0:D], ring[:, slot, k, :], wg[:, k, :], start=k == 0, stop=k == KD - 1)
                    last.then_inc(b_done, 1)
                over_tiles(pe, TILES, 2, product)

                for b in range(2):
                    for m in range(2):
                        last = nc.tensor.transpose(bank[2 + b][0:GB, m * P:(m + 1) * P], bounds[:, m, b * GB:(b + 1) * GB], ident[:, :])
                last.then_inc(b_bt, 1)
                pe.wait_ge(b_bc, 1)
                for m in range(2):
                    for b in range(2):
                        nc.tensor.matmul(bank[4][0:1, m * 256 + b * GB:m * 256 + (b + 1) * GB], bcol[:, b, m:m + 1],
                                         ident[0:GB, 0:GB], start=True, stop=True)
                for b in range(2):
                    nc.tensor.matmul(bank[5][0:1, 0:GROUPS], bcol[:, b, 1:2], upper[:, b, :], start=b == 0, stop=b == 1)
                for b in range(2):
                    last = nc.tensor.matmul(bank[6][:, b * GB:(b + 1) * GB], bcol[:, b, 0:1].to_broadcast([GB, P]),
                                            ident[0:GB, 0:GB], start=True, stop=True)
                last.then_inc(b_br, 1)

            @block.scalar
            def _(act):
                act.sem_inc(b_copied, 2)

                act.sem_inc(b_stored[0], 16)
                act.sem_inc(b_stored[1], 16)

                def rows(t, slot, turn):
                    act.wait_ge(b_done, t + 3)
                    act.wait_ge(b_stored[slot], turn * 16 + 16)
                    nc.scalar.copy(work[:, slot, :], bank[slot][:, 0:D]).then_inc(b_copied, 1)
                with act.Fori(0, TILES // 2) as i:
                    for u in range(2):
                        rows(i * 2 + u, u, i)
                rows(TILES - 1, 0, TILES // 2)

            @block.sync
            def _(sp):
                def store(t, slot):
                    sp.wait_ge(b_copied, t + 3)
                    sp.dma_start(feat_rows[bass.ds(t * P, P), :], work[:, slot, :]).then_inc(b_stored[slot], 16)
                over_tiles(sp, TILES, 2, store)
                sp.wait_ge(b_stored[0], 16 * (TILES // 2 + 2))
                sp.wait_ge(b_stored[1], 16 * (TILES // 2 + 1))

        edge_phase(
            nc, sem, acc=acc, xnT=xnT, src_tab=src_tab, dst_tab=dst_tab, ew_tab=ew_tab, msg=msg, src_row=src_row, same=same,
            onehot=onehot, joined=joined, window=window, rest_onehot=rest_onehot, rest_joined=rest_joined,
            rest_window=rest_window, earlier=earlier, spare=spare, clash=clash, unused=unused, target=target, src_rows=src_rows, wkv=wkv, wq=wq, woT=woT, iota=iota, ones=ones, eps=eps, zeros=zeros, brow=brow,
            ring=ring, sq=sq, k_sb=k_sb, v_sb=v_sb, hs=hs, table=table, dots_sb=dots_sb, pq_sb=pq_sb, mix=mix,
            tiny=tiny, bank=bank, feat_rows=feat_rows, edge_sums=edge_sums, big=edge_area)
        expert_phase(
            nc, sem, acc=acc, yT=xnT, w1=w1, w2=w2, w1_sb=w1_sb, w2_sb=w2_sb, wr=wr, b1_sb=b1_sb, b2_sb=b2_sb, ident=ident,
            eps=eps, work=work, ring=ring, stats=stats, ln=ln, router=router, route1=route1, rank=rank, combT=combT,
            comb1=comb1, bank=bank, out=out, hbuf=onehot)


def row_statistics(link, nc, stats, ln, signal):
    even, odd = stats[:, 0:TILES, 1], stats[:, 0:TILES, 4]
    link(nc.vector.tensor_tensor(ln[:, 0, :], even, odd, ALU.add))
    link(nc.vector.tensor_tensor(ln[:, 3, :], even, odd, ALU.subtract))
    link(nc.vector.tensor_scalar_mul(ln[:, 0, :], ln[:, 0, :], 0.5))
    link(nc.vector.tensor_tensor(ln[:, 4, :], stats[:, 0:TILES, 2], stats[:, 0:TILES, 5], ALU.add))
    link(nc.vector.tensor_tensor(ln[:, 3, :], ln[:, 3, :], ln[:, 3, :], ALU.mult))
    link(nc.vector.tensor_scalar_mul(ln[:, 4, :], ln[:, 4, :], 1.0 / D))
    nc.vector.scalar_tensor_tensor(out=ln[:, 1, :], in0=ln[:, 3, :], scalar=0.25, in1=ln[:, 4, :], op0=ALU.mult,
                                   op1=ALU.add).then_inc(signal, 1)


def edge_phase(nc, sem, *, acc, xnT, src_tab, dst_tab, ew_tab, msg, src_row, same, onehot, joined, window,
               rest_onehot, rest_joined, rest_window, earlier, spare, clash, unused, target, src_rows, wkv, wq, woT,
               iota, ones, eps, zeros, brow, ring, sq, k_sb, v_sb, hs, table, dots_sb, pq_sb, mix, tiny, bank,
               feat_rows, edge_sums, big):
    jbank, mbank, rbank = bank[0], [bank[1], bank[2]], bank[3]
    kb, vb, dots, mm = bank[4], bank[5], bank[6], bank[7]
    QPI = 4
    ITERS = QUADS // QPI

    rows_in = [sem(f"c_sources_loaded{i}") for i in range(2)]
    win_in = [sem(f"c_window_loaded{i}") for i in range(2)]
    rest_in = sem("c_rest_window_loaded")
    same_made = sem("c_same_made")
    built = sem("c_matrices_built")
    idx_ch = sem("c_index_chain")
    j_done = sem("c_joined_ready")
    j_kept = sem("c_joined_kept")
    m_done = sem("c_messages_ready")
    m_kept = sem("c_messages_kept")
    msg_ready = sem("c_messages_complete")
    scattered = [sem(f"c_scattered{r}") for r in range(SUMS)]
    scatter_free = sem("c_former_scatters_done")
    rest_shift = sem("c_rest_shifted")
    rest_ready = sem("c_rest_onehot_ready")
    rest_j = sem("c_rest_joined_ready")
    rest_jk = sem("c_rest_joined_kept")
    rest_m = sem("c_rest_messages_ready")
    rest_added = sem("c_rest_added")
    ring_ready = sem("c_ring_ready")
    kv_done = sem("c_kv_ready")
    sq_done = sem("c_squares_ready")
    k_kept = sem("c_k_kept")
    ss_done = sem("c_square_sums_ready")
    sd_done = sem("c_deviations_ready")
    c_ch = sem("c_vector_chain")
    v_ready = sem("c_v_ready")
    dots_done = sem("c_dots_added")
    dots_kept = sem("c_dots_kept")
    p_done = sem("c_p_ready")
    p_kept = sem("c_p_kept")
    mix_done = sem("c_mix_ready")
    mix_kept = sem("c_mix_kept")
    mm_done = sem("c_mixed_ready")
    mm_added = sem("c_mixed_added")
    act_waits = sem("c_act_waits_passed")
    sp_waits = sem("c_sync_waits_passed")

    def further(eng, g):
        count = eng.value_load(table[0:1, 1, bass.ds(g, 1)], min_val=0, max_val=TILES)
        before = eng.value_load(table[0:1, 2, bass.ds(g, 1)], min_val=0, max_val=2 * GROUPS * TILES)
        return count, before

    with nc.Block() as block:
        @block.sync
        def _(sp):
            def start_row(g):
                return sp.value_load(table[0:1, 0, bass.ds(g, 1)], min_val=0, max_val=N - 1)

            def load(g, h):
                sp.wait_ge(m_done, g * 4 + 4)
                sp.sem_inc(sp_waits, 1)
                sp.dma_start(window[:, h, :], feat_rows[bass.ds(start_row(g), P), :]).then_inc(win_in[h], 16)
                for u in range(2):
                    sp.wait_ge(built, g * 2 + u + 1)
                    sp.sem_inc(sp_waits, 1)
                    row = src_rows[bass.ds((g * 2 + u) * (QT * P), QT * P)].unsqueeze(0).to_broadcast([P, QT * P])
                    sp.dma_start(src_row[:, u, :, :].rearrange("p j e -> p (j e)"), row).then_inc(rows_in[u], 16)

            def rest(g):
                count, before = further(sp, g)
                base = start_row(g)
                with sp.If(0 < count):
                    for u in range(2):
                        with sp.Fori(1, count + 1) as w:
                            n = before + count * u + w
                            sp.wait_ge(rest_added, n * QT)
                            sp.sem_inc(sp_waits, 1)
                            sp.dma_start(rest_window[:, :], feat_rows[bass.ds(nc.s_assert_within(base + w * P, 0, N - 1), P), :]).then_inc(rest_in, 16)

            load(0, 0)
            with sp.Fori(0, ITERS - 1) as i:
                load(i * 2 + 1, 1)
                rest(i * 2)
                load(i * 2 + 2, 0)
                rest(i * 2 + 1)
            load(GROUPS - 1, 1)
            rest(GROUPS - 2)
            rest(GROUPS - 1)

        @block.gpsimd
        def _(pool):
            def scatter(q, slot):
                pool.wait_ge(msg_ready, q + 1)
                pool.sem_inc(pool_waits, 1)
                for j in range(QT):
                    if not isinstance(q, int) or q:
                        pool.wait_ge(scattered[j], q * 16)
                    pool.sem_inc(scatter_free, 1)
                    nc.gpsimd.indirect_dma_start(
                        out=edge_sums[j], out_offset=bass.IndirectOffsetOnAxis(ap=target[:, slot, j:j + 1], axis=0),
                        in_=msg[:, slot, j, :], in_offset=None, compute_op=ALU.add).then_inc(scattered[j], 16)
            pool_waits = sem("c_pool_waits_passed")
            for u in range(QPI):
                scatter(u, u)
            with pool.Fori(1, ITERS) as i:
                for u in range(QPI):
                    scatter(i * QPI + u, u)
            for j in range(QT):
                pool.wait_ge(scattered[j], QUADS * 16)

        @block.tensor
        def _(pe):
            pe.sem_inc(m_done, 8)
            pe.sem_inc(rest_j, QT)
            pe.sem_inc(rest_m, QT)

            def join(q, u):
                pe.wait_ge(built, q + 3)
                pe.wait_ge(j_kept, q + 1)
                for j in range(QT):
                    last = nc.tensor.matmul(jbank[:, j * P:(j + 1) * P], onehot[:, u % 2, j, :], same[:, u % 2, j, :],
                                            start=True, stop=True)
                last.then_inc(j_done, 1)

            def messages(q, u, turn):
                pe.wait_ge(win_in[u // 2], turn * 16 + 16)
                pe.wait_ge(j_kept, q + 2)
                for b in range(2):
                    pe.wait_ge(m_kept, q * 2 + b + 1)
                    for j in range(2):
                        last = nc.tensor.matmul(mbank[b][:, j * D:(j + 1) * D], joined[:, u % 2, 2 * b + j, :],
                                                window[:, u // 2, :], start=True, stop=True)
                    last.then_inc(m_done, 1)

            def rest(q, u, g):
                count, before = further(pe, g)
                with pe.If(0 < count):
                    with pe.Fori(1, count + 1) as w:
                        n = before + count * (u % 2) + w
                        pe.wait_ge(rest_in, n * 16)
                        pe.wait_ge(rest_ready, n)
                        for j in range(QT):
                            pe.wait_ge(rest_added, n * QT + j)
                            nc.tensor.matmul(rbank[:, 0:P], rest_onehot[:, j, :], same[:, u % 2, j, :],
                                             start=True, stop=True).then_inc(rest_j, 1)
                            pe.wait_ge(rest_jk, n * QT + j + 1)
                            nc.tensor.matmul(rbank[:, D:2 * D], rest_joined[:, :], rest_window[:, :],
                                             start=True, stop=True).then_inc(rest_m, 1)

            def attend(i):
                pe.wait_ge(ring_ready, i + 1)
                pe.wait_ge(k_kept, i + 1)
                pe.wait_ge(v_ready, i + 1)
                for c, b in ((0, kb), (1, vb)):
                    for k in range(KD):
                        last = nc.tensor.matmul(b[:, :], ring[:, 0, k, :], wkv[:, k, c * INNER:(c + 1) * INNER],
                                                start=k == 0, stop=k == KD - 1)
                last.then_inc(kv_done, 1)

            def dot(i):
                pe.wait_ge(v_ready, i + 2)
                pe.wait_ge(k_kept, i + 2)
                for q in range(PAIRS):
                    last = nc.tensor.matmul(dots[:, q * P:(q + 1) * P], v_sb[:, 2 * q:2 * q + 2, :].rearrange("p h c -> p (h c)"),
                                            k_sb[:, q * P:(q + 1) * P], start=False, stop=False, skip_group_check=True)
                last.then_inc(dots_done, 1)

            def mixed(i):
                pe.wait_ge(ring_ready, i + 1)
                pe.wait_ge(mm_added, i + 1 - TILES)
                for k in range(KD):
                    nc.tensor.matmul(mm[:, 0:D], ring[:, 0, k, :], mix[:, k, :], start=k == 0, stop=False)
                nc.tensor.matmul(mm[:, 0:D], ones[0:1, :], brow[0:1, 2, :], start=False, stop=True).then_inc(mm_done, 1)

            def former(i, u):
                if u:
                    messages(i * QPI + u - 1, u - 1, i)
                    rest(i * QPI + u - 1, u - 1, i * 2 + (u - 1) // 2)
                else:
                    messages(i * QPI - 1, QPI - 1, i - 1)
                    rest(i * QPI - 1, QPI - 1, i * 2 - 1)

            def step(i, before=None, after=None):
                if before:
                    before(i)
                for u in range(QPI):
                    join(i * QPI + u, u)
                    if u or not isinstance(i, int) or i:
                        former(i, u)
                if after:
                    after(i)

            nc.tensor.matmul(dots[:, :], zeros[:, 0:P], wkv[:, 0, 0:512], start=True, stop=False, skip_group_check=True)
            step(0, attend, dot)
            with pe.Fori(1, TILES) as i:
                step(i, attend, dot)
            nc.tensor.matmul(dots[:, :], zeros[:, 0:P], wkv[:, 0, 0:512], start=False, stop=True,
                             skip_group_check=True).then_inc(dots_done, 1)

            pe.wait_ge(dots_kept, 1)
            for q in range(PAIRS):
                b = (kb, vb)[q % 2]
                if q >= 2:
                    pe.wait_ge(p_kept, q - 1)
                nc.tensor.matmul(b[:, 0:D], dots_sb[:, q, :], woT[:, q, :], start=True, stop=True).then_inc(p_done, 1)
            pe.wait_ge(p_kept, PAIRS)
            for k in range(KD):
                for q in range(PAIRS):
                    last = nc.tensor.matmul(mm[:, k * D:(k + 1) * D], wq[:, q, k * P:(k + 1) * P], pq_sb[:, q, :],
                                            start=q == 0, stop=q == PAIRS - 1)
            last.then_inc(mix_done, 1)
            pe.wait_ge(mix_kept, 1)
            with pe.Fori(TILES, 2 * TILES) as i:
                step(i, mixed)
            with pe.Fori(2 * TILES, ITERS) as i:
                step(i)
            former(ITERS, 0)

        @block.scalar
        def _(act):
            act.sem_inc(k_kept, 1)
            act.sem_inc(j_kept, 1)
            act.sem_inc(m_kept, 2)

            def keep_joined(q, u):
                act.wait_ge(j_done, q + 1)
                nc.scalar.copy(joined[:, u % 2, :, :].rearrange("p j e -> p (j e)"), jbank[:, :]).then_inc(j_kept, 1)

            def rows(q, u):
                act.wait_ge(scatter_free, q * 4 + 8)
                for b in range(2):
                    act.wait_ge(m_done, q * 2 + b + 9)
                    nc.scalar.copy(msg[:, u, 2 * b:2 * b + 2, :].rearrange("p j d -> p (j d)"), mbank[b][:, :]).then_inc(m_kept, 1)

            def keys(i):
                act.wait_ge(kv_done, i + 1)
                nc.scalar.activation(sq[:, 0, :, :].rearrange("p h c -> p (h c)"), kb[:, :], ACT.Square)
                nc.scalar.activation(sq[:, 1, :, :].rearrange("p h c -> p (h c)"), vb[:, :], ACT.Square).then_inc(sq_done, 1)
                act.wait_ge(dots_done, i + 1)
                nc.scalar.copy(k_sb[:, :], kb[:, :]).then_inc(k_kept, 1)

            def deviations(i):
                act.wait_ge(ss_done, i + 1)
                nc.scalar.activation(hs[:, 1, :], hs[:, 0, :], ACT.Sqrt, bias=eps[:, :], scale=1.0 / DH).then_inc(sd_done, 1)

            def operand(t):
                nc.scalar.copy(ring[:, 0, :, :], xnT[:, :, bass.ds(t * P, P)]).then_inc(ring_ready, 1)

            def attention(i, u):
                if u == 0:
                    keys(i)
                    operand(i + 1)
                if u == 1:
                    deviations(i)

            def mixing(i, u):
                if u == 0:
                    act.wait_ge(mm_done, i + 1 - TILES)
                    act.sem_inc(act_waits, 1)
                    operand(i + 1 - TILES)

            def step(i, other=None):
                for u in range(QPI):
                    keep_joined(i * QPI + u, u)
                    if u:
                        rows(i * QPI + u - 1, u - 1)
                    elif not isinstance(i, int) or i:
                        rows(i * QPI - 1, QPI - 1)
                    if other:
                        other(i, u)

            def last_attention(i, u):
                if u == 0:
                    keys(i)
                if u == 1:
                    deviations(i)

            operand(0)
            step(0, attention)
            with act.Fori(1, TILES - 1) as i:
                step(i, attention)
            step(TILES - 1, last_attention)
            for q in range(PAIRS):
                act.wait_ge(p_done, q + 1)
                nc.scalar.copy(pq_sb[:, q, :], (kb, vb)[q % 2][:, 0:D]).then_inc(p_kept, 1)
            act.wait_ge(mix_done, 1)
            nc.scalar.copy(mix[:, :, :], mm[:, :].rearrange("p (k d) -> p k d", k=KD)).then_inc(mix_kept, 1)
            operand(0)
            with act.Fori(TILES, 2 * TILES - 1) as i:
                step(i, mixing)
            with act.Fori(2 * TILES - 1, ITERS) as i:
                step(i)
            rows(QUADS - 1, QPI - 1)

        @block.vector
        def _(dve):
            dve.sem_inc(scatter_free, 16)
            dve.sem_inc(built, 2)
            dve.sem_inc(rest_jk, QT)
            dve.sem_inc(rest_added, QT)
            dve.sem_inc(v_ready, 1)
            dve.sem_inc(dots_done, 1)
            dve.sem_inc(mm_added, 1)

            def one_hot(to, q, signal):
                for j in range(QT):
                    last = nc.vector.tensor_scalar(to[:, j, :], iota[:, :], dst_tab[:, bass.ds(q * QT + j, 1)],
                                                   ew_tab[:, bass.ds(q * QT + j, 1)], ALU.is_equal, ALU.mult)
                last.then_inc(signal, 1)

            def build(i, u):
                q = i * QPI + u
                dve.wait_ge(rows_in[u % 2], i * 32 + (u // 2) * 16 + 16)
                for j in range(QT):
                    last = nc.vector.tensor_scalar(same[:, u % 2, j, :], src_row[:, u % 2, j, :],
                                                   src_tab[:, bass.ds(q * QT + j, 1)], None, ALU.is_equal)
                last.then_inc(same_made, 1)
                one_hot(onehot[:, u % 2, :, :], q, built)
                dve.wait_ge(same_made, q + 1)
                dve.wait_ge(scatter_free, q * 4 + 8)
                link = Chain(dve, idx_ch, q * 3)
                clashes, hit, off = (clash[:, u, n, :] for n in range(3))
                for j in range(QT):
                    last = nc.vector.tensor_tensor_reduce(out=unused[:, j, :], in0=same[:, u % 2, j, :], in1=earlier[:, :],
                                                          scale=1.0, scalar=0.0, op0=ALU.mult, op1=ALU.add,
                                                          accum_out=clashes[:, j:j + 1])
                link(last)
                link(nc.vector.tensor_scalar_min(hit, clashes, 1.0))
                sources = src_tab[:, bass.ds(q * QT, QT)]
                link(nc.vector.scalar_tensor_tensor(out=off, in0=sources, scalar=spare[:, :], in1=hit,
                                                    op0=ALU.subtract, op1=ALU.mult))
                nc.vector.tensor_tensor(target[:, u, :], sources, off, ALU.subtract)

            def finish(q, u, g):
                count, before = further(dve, g)
                with dve.If(0 < count):
                    with dve.Fori(1, count + 1) as w:
                        n = before + count * (u % 2) + w
                        at = dst_tab[:, bass.ds(q * QT, QT)]
                        nc.vector.tensor_scalar_add(at, at, -float(P)).then_inc(rest_shift, 1)
                        dve.wait_ge(rest_shift, n)
                        one_hot(rest_onehot, q, rest_ready)
                        for j in range(QT):
                            dve.wait_ge(rest_j, n * QT + j + 1)
                            nc.vector.tensor_copy(rest_joined[:, :], rbank[:, 0:P]).then_inc(rest_jk, 1)
                            dve.wait_ge(rest_m, n * QT + j + 1)
                            if j == 0:
                                dve.wait_ge(m_kept, q * 2 + 4)
                            nc.vector.tensor_tensor(msg[:, u, j, :], msg[:, u, j, :], rbank[:, D:2 * D], ALU.add
                                                    ).then_inc(rest_added, 1)
                dve.wait_ge(m_kept, q * 2 + 4)
                nc.vector.memset(tiny[:, u:u + 1], 0.0).then_inc(msg_ready, 1)

            def values(i, u):
                if u == 1:
                    dve.wait_ge(sq_done, i + 1)
                    nc.vector.tensor_reduce(hs[:, 0, :], sq[:, :, :, :].rearrange("p a h c -> p (a h) c"), AX.X,
                                            ALU.add).then_inc(ss_done, 1)
                if u == 2:
                    link = Chain(dve, c_ch, i * 2)
                    dve.wait_ge(sd_done, i + 1)
                    link(nc.vector.reciprocal(hs[:, 2, :], hs[:, 1, :]))
                    link(nc.vector.tensor_tensor(hs[:, 2, 0:HEADS], hs[:, 2, 0:HEADS], hs[:, 2, HEADS:], ALU.mult))
                    dve.wait_ge(dots_done, i + 1)
                    nc.vector.tensor_tensor(v_sb[:, :, :], vb[:, :].rearrange("p (h c) -> p h c", h=HEADS),
                                            hs[:, 2, 0:HEADS].unsqueeze(2).to_broadcast([P, HEADS, DH]), ALU.mult).then_inc(v_ready, 1)

            def mixed(i, u):
                if u == 1:
                    dve.wait_ge(mm_done, i + 1 - TILES)
                    to = acc[:, bass.ds(i - TILES, 1), :].rearrange("p t d -> p (t d)")
                    nc.vector.tensor_tensor(to, to, mm[:, 0:D], ALU.add).then_inc(mm_added, 1)

            def step(i, other=None):
                for u in range(QPI):
                    build(i, u)
                    if u:
                        finish(i * QPI + u - 1, u - 1, i * 2 + (u - 1) // 2)
                    elif not isinstance(i, int) or i:
                        finish(i * QPI - 1, QPI - 1, i * 2 - 1)
                    if other:
                        other(i, u)

            step(0, values)
            with dve.Fori(1, TILES) as i:
                step(i, values)
            dve.wait_ge(dots_done, TILES + 2)
            for h in range(2):
                blk = dots_sb[h * DH:(h + 1) * DH, :, h * DH:(h + 1) * DH]
                last = nc.vector.tensor_scalar_mul(blk, dots[h * DH:(h + 1) * DH, :].rearrange("p (q d) -> p q d", q=PAIRS)[
                    :, :, h * DH:(h + 1) * DH], 1.0 / N)
            last.then_inc(dots_kept, 1)
            with dve.Fori(TILES, 2 * TILES) as i:
                step(i, mixed)
            with dve.Fori(2 * TILES, ITERS) as i:
                step(i)
            finish(QUADS - 1, QPI - 1, GROUPS - 1)

    CT = 7
    loaded = [sem(f"d_sum_loaded{r}") for r in range(SUMS)]
    used = sem("d_sum_added")
    parts = [big[:, r * CT * D:(r + 1) * CT * D].rearrange("p (t d) -> p t d", t=CT) for r in range(SUMS)]
    with nc.Block() as block:
        @block.sync
        def _(sp):
            with sp.Fori(0, TILES // CT) as c:
                for r in range(SUMS):
                    sp.wait_ge(used, c * SUMS + r + 1)
                    sp.dma_start(parts[r], edge_sums[r][bass.ds(c * (CT * P), CT * P), :].rearrange("(t p) d -> p t d", p=P)
                                 ).then_inc(loaded[r], 16)

        @block.vector
        def _(dve):
            dve.sem_inc(used, SUMS)
            with dve.Fori(0, TILES // CT) as c:
                for r in range(SUMS):
                    dve.wait_ge(loaded[r], c * 16 + 16)
                    dve.wait_ge(used, c * SUMS + r + SUMS)
                    to = acc[:, bass.ds(c * CT, CT), :]
                    nc.vector.tensor_tensor(to, to, parts[r], ALU.add).then_inc(used, 1)


def expert_phase(nc, sem, *, acc, yT, w1, w2, w1_sb, w2_sb, wr, b1_sb, b2_sb, ident, eps, work, ring, stats, ln,
                 router, route1, rank, combT, comb1, bank, out, hbuf):
    w_in = sem("e_expert_weights_loaded")
    ch = sem("e_vector_chain")
    var = sem("e_variance_ready")
    std = sem("e_deviation_ready")
    row = sem("e_row_ready")
    turned = sem("e_row_turned")
    kept = sem("e_row_kept")
    ringed = sem("e_operand_ready")
    logit = sem("e_logits_ready")
    logit_kept = sem("e_logits_kept")
    shifted = sem("e_logits_shifted")
    exped = sem("e_exponentials_ready")
    probs, one1, one2, tmp, comb = (router[:, i, :, :] for i in range(5))
    top, top2, den, inv = (route1[:, i, :] for i in range(4))

    def wide(a):
        return a.unsqueeze(2).to_broadcast([P, TILES, EXPERTS])

    with nc.Block() as block:
        @block.sync
        def _(sp):
            sp.dma_start(w1_sb, w1.rearrange("e (k p) n -> p e k n", p=P)).then_inc(w_in, 16)
            sp.dma_start(w2_sb, w2.rearrange("e (k p) n -> p e k n", p=P)).then_inc(w_in, 16)
            sp.wait_ge(w_in, 32)

        @block.vector
        def _(dve):
            link = Chain(dve, ch)
            for t in range(TILES):
                last = nc.vector.bn_stats(stats[:, t, :], acc[:, t, :])
            link(last)
            row_statistics(link, nc, stats, ln, var)
            dve.wait_ge(std, 1)
            link(nc.vector.reciprocal(ln[:, 1, :], ln[:, 2, :]))

            def logits(t, slot):
                dve.wait_ge(logit, t + 1)
                nc.vector.tensor_copy(router[:, 0, bass.ds(t, 1), :].rearrange("p t e -> p (t e)"),
                                      bank[2 + slot][:, 0:EXPERTS]).then_inc(logit_kept, 1)

            def step(t, slot):
                dve.wait_ge(turned, t + 1)
                src = acc[:, bass.ds(t, 1), :].rearrange("p t d -> p (t d)")
                nc.vector.tensor_scalar(work[:, slot, :], src, ln[:, 0, bass.ds(t, 1)], ln[:, 1, bass.ds(t, 1)],
                                        ALU.subtract, ALU.mult).then_inc(row, 1)

            def keep(t, slot):
                dve.wait_ge(turned, t + 3)
                dve.wait_ge(kept, t + 1)
                nc.vector.tensor_copy(ring[:, slot, :, :], bank[slot][:, 0:D].rearrange("p (k n) -> p k n", k=KD)
                                      ).then_inc(ringed, 1)
                src = acc[:, bass.ds(t, 1), :].rearrange("p t d -> p (t d)")
                nc.vector.tensor_tensor(src, src, work[:, slot, :], ALU.add)
            dve.sem_inc(logit_kept, 2)

            def both(t, slot):
                step(t, slot)
                keep(t, slot)
                logits(t, slot)
            over_tiles(dve, TILES, 2, both)

            dve.wait_ge(logit_kept, TILES + 2)
            link(nc.vector.tensor_reduce(top, probs, AX.X, ALU.max))
            nc.vector.tensor_tensor(tmp, probs, wide(top), ALU.subtract).then_inc(shifted, 1)
            dve.wait_ge(exped, 1)
            link(nc.vector.tensor_reduce(den, comb, AX.X, ALU.add))
            link(nc.vector.reciprocal(inv, den))
            link(nc.vector.tensor_tensor(probs, comb, wide(inv), ALU.mult))
            by_rank = rank[:, :].unsqueeze(1).to_broadcast([P, TILES, EXPERTS])
            for n, (best, one) in enumerate(((top, one1), (top2, one2))):
                of = probs if n == 0 else comb
                link(nc.vector.tensor_reduce(best, of, AX.X, ALU.max))
                link(nc.vector.tensor_tensor(tmp, of, wide(best), ALU.is_equal))
                link(nc.vector.tensor_tensor(tmp, tmp, by_rank, ALU.mult))
                link(nc.vector.tensor_reduce(den, tmp, AX.X, ALU.max))
                link(nc.vector.tensor_tensor(one, tmp, wide(den), ALU.is_equal))
                if n == 0:
                    link(nc.vector.scalar_tensor_tensor(out=comb, in0=one, scalar=-2.0, in1=probs, op0=ALU.mult, op1=ALU.add))
            link(nc.vector.tensor_tensor(den, top, top2, ALU.add))
            link(nc.vector.tensor_scalar_max(den, den, 1e-12))
            link(nc.vector.reciprocal(inv, den))
            link(nc.vector.tensor_tensor(tmp, one1, one2, ALU.add))
            link(nc.vector.tensor_tensor(tmp, tmp, probs, ALU.mult))
            link(nc.vector.tensor_tensor(comb, tmp, wide(inv), ALU.mult))

        @block.tensor
        def _(pe):
            pe.sem_inc(turned, 2)

            def turn(t, slot):
                pe.wait_ge(row, t + 1)
                pe.wait_ge(ringed, t + 1)
                for k in range(KD):
                    last = nc.tensor.transpose(bank[slot][:, k * P:(k + 1) * P], work[:, slot, k * P:(k + 1) * P], ident[:, :])
                last.then_inc(turned, 1)

                pe.wait_ge(ringed, t + 3)
                pe.wait_ge(logit_kept, t + 1)
                for k in range(KD):
                    last = nc.tensor.matmul(bank[2 + slot][:, 0:EXPERTS], ring[:, slot, k, :], wr[:, k, :],
                                            start=k == 0, stop=k == KD - 1)
                last.then_inc(logit, 1)
            pe.sem_inc(ringed, 2)
            over_tiles(pe, TILES, 2, turn)

        @block.scalar
        def _(act):
            act.wait_ge(var, 1)
            nc.scalar.activation(ln[:, 2, :], ln[:, 1, :], ACT.Sqrt, bias=eps[:, :]).then_inc(std, 1)
            act.sem_inc(kept, 2)

            def keep(t, slot):
                act.wait_ge(ringed, t + 3)
                nc.scalar.copy(yT[:, :, bass.ds(t * P, P)], ring[:, slot, :, :]).then_inc(kept, 1)
            over_tiles(act, TILES, 2, keep)
            act.wait_ge(shifted, 1)
            nc.scalar.activation(comb, tmp, ACT.Exp).then_inc(exped, 1)

    c_staged = sem("f_weights_staged")
    c_turned = sem("f_weights_turned")
    c_kept = sem("f_weights_kept")
    l1_done = sem("f_hidden_ready")
    gelued = sem("f_gelu_ready")
    l2_done = sem("f_output_ready")
    added = sem("f_output_added")
    b_done = sem("f_bias_ready")
    bias_added = sem("f_bias_added")
    stored = sem("f_stored")
    dve_waits = sem("f_vector_waits_passed")
    hp = [bank[0], bank[1]]
    op = [bank[2], bank[3]]
    ctb, bb = bank[4], bank[5]
    hidden = [hbuf[:, s, 0:KD, :] for s in range(2)]
    with nc.Block() as block:
        @block.tensor
        def _(pe):
            def layer1(t, e):
                n = t * EXPERTS + e
                pe.wait_ge(gelued, n + 1)
                for h in range(KD):
                    for k in range(KD):
                        last = nc.tensor.matmul(hp[e % 2][:, h * P:(h + 1) * P], w1_sb[:, e, k, h * P:(h + 1) * P],
                                                yT[:, k, bass.ds(t * P, P)], start=k == 0, stop=k == KD - 1)
                last.then_inc(l1_done, 1)

            def layer2(t, e):
                n = t * EXPERTS + e
                pe.wait_ge(gelued, n + 3)
                pe.wait_ge(added, n + 1)
                for k in range(KD):
                    last = nc.tensor.matmul(op[e % 2][:, 0:D], hidden[e % 2][:, k, :], w2_sb[:, e, k, :], start=k == 0, stop=k == KD - 1)
                last.then_inc(l2_done, 1)

            def biases(t):
                pe.wait_ge(c_staged, t + 1)
                nc.tensor.transpose(ctb[0:EXPERTS, 0:P], comb1[:, :], ident[:, :]).then_inc(c_turned, 1)

            def biases2(t):
                pe.wait_ge(c_kept, t + 1)
                nc.tensor.matmul(bb[:, 0:D], combT[:, :], b2_sb[:, :], start=True, stop=True).then_inc(b_done, 1)

            def tile(t, more):
                biases(t)
                for e in range(EXPERTS):
                    if e + 1 < EXPERTS:
                        layer1(t, e + 1)
                    elif more:
                        layer1(t + 1, 0)
                    if e == 2:
                        biases2(t)
                    layer2(t, e)
            layer1(0, 0)
            with pe.Fori(0, TILES - 1) as t:
                tile(t, True)
            tile(TILES - 1, False)

        @block.scalar
        def _(act):
            act.sem_inc(gelued, 2)
            act.sem_inc(l2_done, 2)
            with act.Fori(0, TILES) as t:
                for e in range(EXPERTS):
                    n = t * EXPERTS + e
                    act.wait_ge(l1_done, n + 1)
                    act.wait_ge(l2_done, n + 1)
                    for h in range(KD):
                        last = nc.scalar.activation(hidden[e % 2][:, h, :], hp[e % 2][:, h * P:(h + 1) * P], ACT.Gelu,
                                                    bias=b1_sb[:, e, h:h + 1])
                    last.then_inc(gelued, 1)

        @block.vector
        def _(dve):
            dve.sem_inc(added, 2)

            def tile(t, slot):
                nc.vector.tensor_copy(comb1[:, :], router[:, 4, bass.ds(t, 1), :].rearrange("p t e -> p (t e)")
                                      ).then_inc(c_staged, 1)
                dve.wait_ge(c_turned, t + 1)
                nc.vector.tensor_copy(combT[:, :], ctb[0:EXPERTS, 0:P]).then_inc(c_kept, 1)
                to = acc[:, bass.ds(t, 1), :].rearrange("p t d -> p (t d)")
                last = None
                for e in range(EXPERTS):
                    n = t * EXPERTS + e
                    dve.wait_ge(added, n + 2)
                    if e == 4:
                        dve.wait_ge(b_done, t + 1)
                        nc.vector.tensor_tensor(to, to, bb[:, 0:D], ALU.add).then_inc(bias_added, 1)
                        dve.wait_ge(bias_added, t + 1)
                    dve.wait_ge(l2_done, n + 3)
                    last = nc.vector.scalar_tensor_tensor(out=to, in0=op[e % 2][:, 0:D],
                                                          scalar=router[:, 4, bass.ds(t, 1), e:e + 1].rearrange("p t e -> p (t e)"),
                                                          in1=to, op0=ALU.mult, op1=ALU.add)
                    last.then_inc(added, 1)
            over_tiles(dve, TILES, 1, tile)

        @block.sync
        def _(sp):
            with sp.Fori(0, FULL) as t:
                sp.wait_ge(added, t * EXPERTS + EXPERTS + 2)
                sp.dma_start(out[bass.ds(t * P, P), :], acc[:, bass.ds(t, 1), :].rearrange("p t d -> p (t d)")).then_inc(stored, 16)
            sp.wait_ge(added, TILES * EXPERTS + 2)
            sp.dma_start(out[FULL * P:N, :], acc[0:LAST, FULL, :]).then_inc(stored, 16)
            sp.wait_ge(stored, 16 * TILES)


def kernel(**inputs):
    import numpy as np
    import concourse.bacc as bacc
    from concourse.bass_utils import run_bass_kernel_spmd

    def a(name):
        return np.ascontiguousarray(inputs[name])

    def grouped(v):
        return np.concatenate([v[:(GROUPS - 1) * GE], v[EDGES - GE:]])

    def by_partition(v):
        return np.ascontiguousarray(grouped(v).reshape(COLS, P).T)

    qkv = a("L0_mix_w_qkv")
    arrays = {
        "x": a("x"), "src": by_partition(a("src")), "dst": by_partition(a("dst")), "ew": by_partition(a("edge_weight")),
        "src_rows": grouped(a("src")),
        "w_gnn": a("L0_gnn_weight"), "b_gnn": a("L0_gnn_bias").reshape(1, D),
        "w_kvT": np.ascontiguousarray(qkv[INNER:].T), "w_q": np.ascontiguousarray(qkv[:INNER]),
        "w_outT": np.ascontiguousarray(a("L0_mix_w_out").T), "b_out": a("L0_mix_b_out").reshape(1, D),
        "w_routerT": np.ascontiguousarray(a("L0_ffn_router_w").T), "w1": a("L0_ffn_w1"),
        "b1T": np.ascontiguousarray(a("L0_ffn_b1").reshape(EXPERTS, KD, P).transpose(2, 0, 1)), "w2": a("L0_ffn_w2"), "b2": a("L0_ffn_b2"),
    }
    nc = bacc.Bacc("TRN2", target_bir_lowering=False, num_devices=1)
    args = [nc.dram_tensor(f"in_{n}", v.shape, mybir.dt.from_np(v.dtype), kind="ExternalInput").ap() for n, v in arrays.items()]
    out = nc.dram_tensor("out_0", (N, D), F32, kind="ExternalOutput").ap()
    build(nc, *args, out)
    r = run_bass_kernel_spmd(nc, [{f"in_{n}": v for n, v in arrays.items()}], core_ids=[0])
    return r.results[0]["out_0"]
```

```python
import concourse.bass as bass
from concourse import mybir
from contextlib import ExitStack

F32 = mybir.dt.float32
I32 = mybir.dt.int32
ALU = mybir.AluOpType
ACT = mybir.ActivationFunctionType
AX = mybir.AxisListType

P = 128
N = 6250
D = 256
KD = D // P
TILES = -(-N // P)
FULL = N // P
LAST = N - FULL * P
NPAD = TILES * P
EDGES = 206250
EPT = 8
QT = 4
GE = EPT * P
GROUPS = -(-EDGES // GE)
REPEATED = GROUPS * GE - EDGES
COLS = GROUPS * EPT
QUADS = COLS // QT
SUMS = 2 * QT
ROWS = TILES * P + P
HEADS, DH = 8, 64
INNER = HEADS * DH
PAIRS = HEADS // 2
EXPERTS = 8
EPS = 1e-5
GB = GROUPS // 2
CH = 250
CHUNKS = N // CH


class Chain:

    def __init__(self, eng, sem, base=0):
        self.eng, self.sem, self.base, self.n = eng, sem, base, 0

    def __call__(self, ins):
        self.n += 1
        ins.then_inc(self.sem, 1)
        self.eng.wait_ge(self.sem, self.base + self.n)


def over_tiles(eng, count, unroll, body):
    rounds = count // unroll
    with eng.Fori(0, rounds) as i:
        for u in range(unroll):
            body(i * unroll + u, u)
    for t in range(rounds * unroll, count):
        body(t, t % unroll)


def build(nc, x, src, dst, ew, src_rows, w_gnn, b_gnn, w_kvT, w_q, w_outT, b_out,
          w_routerT, w1, b1T, w2, b2, out):
    ctx = ExitStack()
    with ctx:
        def sb(name, shape, dt=F32):
            return ctx.enter_context(nc.sbuf_tensor(name, shape, dt))

        def ps(name, shape):
            return ctx.enter_context(nc.psum_tensor(name, shape, F32))

        def sem(name):
            return ctx.enter_context(nc.semaphore(name))

        feat_rows = nc.dram_tensor("feat_rows", (ROWS, D), F32).ap()
        edge_sums = [nc.dram_tensor(f"edge_sums{r}", (ROWS, D), F32).ap() for r in range(SUMS)]

        acc = sb("acc", [P, TILES, D])
        xnT = sb("xnT", [P, KD, NPAD])
        edge_area = sb("edge_area", [P, 3 * COLS + 4 * QT * D])
        src_tab = edge_area[:, 0:COLS]
        dst_tab = edge_area[:, COLS:2 * COLS]
        ew_tab = edge_area[:, 2 * COLS:3 * COLS]
        msg = edge_area[:, 3 * COLS:].rearrange("p (s j d) -> p s j d", s=4, j=QT)
        raw = [edge_area[:, (3 + i) * COLS:(4 + i) * COLS].bitcast(I32) for i in range(2)]
        w1_sb = edge_area[:, 0:EXPERTS * KD * D].rearrange("p (e k n) -> p e k n", e=EXPERTS, k=KD)
        w2_sb = edge_area[:, EXPERTS * KD * D:2 * EXPERTS * KD * D].rearrange("p (e k n) -> p e k n", e=EXPERTS, k=KD)
        src_row = sb("src_row", [P, 4, QT, P], I32)
        same = sb("same", [P, 4, QT, P])
        onehot = sb("onehot", [P, 2, QT, P])
        joined = sb("joined", [P, 2, QT, P])
        window = sb("window", [P, 2, D])
        work = sb("work", [P, 2, D])
        earlier = sb("earlier", [P, P])
        spare = sb("spare", [P, 1])
        unused = sb("unused", [P, QT, P], mybir.dt.bfloat16)
        clash = sb("clash", [P, 4, 3, QT])
        target = sb("target", [P, 4, QT], I32)
        wkv = sb("wkv", [P, KD, 2 * INNER])
        wq = sb("wq", [P, PAIRS, D])
        woT = sb("woT", [P, PAIRS, D])
        wg = joined[:, 0, :, :].rearrange("p j e -> p (j e)").rearrange("p (k d) -> p k d", k=KD)
        wr = sb("wr", [P, KD, EXPERTS])
        b1_sb = sb("b1_sb", [P, EXPERTS, KD])
        b2_sb = sb("b2_sb", [EXPERTS, D])
        ident = sb("ident", [P, P])
        iota = sb("iota", [P, P])
        ones = sb("ones", [P, P])
        eps = sb("eps", [P, 1])
        zeros = sb("zeros", [P, D])
        brow = sb("brow", [1, 3, D])
        ring = sb("ring", [P, 2, KD, P])
        sq = sb("sq", [P, 2, HEADS, DH])
        k_sb = sb("k_sb", [P, INNER])
        v_sb = sb("v_sb", [P, HEADS, DH])
        hs = sb("hs", [P, 3, 2 * HEADS])
        stats = sb("stats", [P, 2 * CHUNKS, 6])
        ln = sb("ln", [P, 6, TILES])
        fm = sb("fm", [P, KD, 4])
        bounds = sb("bounds", [P, 2, GROUPS])
        bcol = sb("bcol", [GB, 2, 2])
        bcol_i = sb("bcol_i", [GB, 2, 1], I32)
        table = sb("table", [1, GROUPS + 1], I32)
        dots_sb = sb("dots_sb", [P, PAIRS, P])
        pq_sb = sq[:, :, :, :].rearrange("p a h c -> p (a h c)").rearrange("p (q d) -> p q d", q=PAIRS)
        mix = sb("mix", [P, KD, D])
        tiny = sb("tiny", [1, 4])
        router = wkv[:, :, :].rearrange("p k n -> p (k n)")[:, 0:5 * TILES * EXPERTS].rearrange(
            "p (a t e) -> p a t e", a=5, t=TILES)
        route1 = sb("route1", [P, 4, TILES])
        rank = sb("rank", [P, EXPERTS])
        combT = sb("combT", [EXPERTS, P])
        comb1 = sb("comb1", [P, EXPERTS])

        bank = [ps(f"bank{i}", [P, 512]) for i in range(8)]

        s_x = [sem(f"x_loaded{i}") for i in range(5)]
        s_w = sem("weights_loaded")
        s_dst = sem("dst_loaded")
        s_pad = sem("pad_cleared")
        s_const = sem("constants_made")
        s_zero = sem("sums_cleared")
        LOADS = 10
        s_ch = sem("a_vector_chain")
        s_pch = sem("a_pool_chain")
        s_var = sem("a_variance_ready")
        s_std = sem("a_deviation_ready")
        s_row = sem("a_row_ready")
        s_turn = sem("a_row_turned")
        s_kept = sem("a_row_kept")
        XC = 12
        with nc.Block() as block:
            @block.sync
            def _(sp):
                for c in range(FULL // XC):
                    sp.dma_start(acc[:, c * XC:(c + 1) * XC, :],
                                 x[c * XC * P:(c + 1) * XC * P, :].rearrange("(t p) d -> p t d", p=P)).then_inc(s_x[c], 16)
                sp.wait_ge(s_pad, 1)
                sp.dma_start(acc[0:LAST, FULL, :], x[FULL * P:N, :]).then_inc(s_x[4], 16)
                sp.dma_start(raw[0], dst).then_inc(s_dst, 16)
                sp.dma_start(raw[1], src).then_inc(s_dst, 16)
                n = 0
                for to, of in ((wkv[:, :, :], w_kvT.rearrange("(k p) e -> p k e", p=P)),
                               (ew_tab, ew),
                               (wg[:, :, :], w_gnn.rearrange("(k p) e -> p k e", p=P)),
                               (wq[:, :, :], w_q.rearrange("(k p) e -> p k e", p=P)),
                               (woT[:, :, :], w_outT.rearrange("(k p) e -> p k e", p=P)),
                               (wr[:, :, :], w_routerT.rearrange("(k p) e -> p k e", p=P)),
                               (b1_sb[:, :, :], b1T),
                               (b2_sb[:, :], b2),
                               (brow[:, 0, :], b_gnn), (brow[:, 1, :], b_out)):
                    sp.dma_start(to, of).then_inc(s_w, 16)
                    n += 16
                assert n == 16 * LOADS
                sp.wait_ge(s_pad, 2)
                for to in edge_sums:
                    sp.dma_start(to.rearrange("(t p) d -> p t d", p=P),
                                 zeros[:, :].unsqueeze(1).to_broadcast([P, ROWS // P, D])).then_inc(s_zero, 16)
                sp.dma_start(feat_rows[NPAD:ROWS, :], zeros[:, :]).then_inc(s_zero, 16)
                sp.wait_ge(s_w, n)
                sp.wait_ge(s_dst, 32)

            @block.gpsimd
            def _(pool):
                link = Chain(pool, s_pch)
                link(nc.gpsimd.memset(ident[:, :], 0.0))
                nc.gpsimd.affine_select(out=ident[:, :], in_=ident[:, :], compare_op=ALU.not_equal, fill=1.0, base=0,
                                        pattern=[[-1, P]], channel_multiplier=1).then_inc(s_const, 1)
                nc.gpsimd.iota(iota[:, :], pattern=[[1, P]], base=0, channel_multiplier=0,
                               allow_small_or_imprecise_dtypes=True).then_inc(s_const, 1)
                nc.gpsimd.iota(rank[:, :], pattern=[[-1, EXPERTS]], base=EXPERTS, channel_multiplier=0,
                               allow_small_or_imprecise_dtypes=True).then_inc(s_const, 1)
                pool.wait_ge(s_w, 16 * LOADS)
                tail = ew_tab[:, COLS - EPT:COLS]
                nc.gpsimd.affine_select(out=tail, in_=tail, compare_op=ALU.is_ge, fill=0.0, base=-REPEATED,
                                        pattern=[[P, EPT]], channel_multiplier=1).then_inc(s_const, 1)
                link(nc.gpsimd.memset(earlier[:, :], 1.0))
                nc.gpsimd.affine_select(out=earlier[:, :], in_=earlier[:, :], compare_op=ALU.is_gt, fill=0.0, base=0,
                                        pattern=[[-1, P]], channel_multiplier=1).then_inc(s_const, 1)
                nc.gpsimd.iota(spare[:, :], pattern=[[0, 1]], base=N, channel_multiplier=1,
                               allow_small_or_imprecise_dtypes=True).then_inc(s_const, 1)

            @block.vector
            def _(dve):
                nc.vector.memset(acc[:, FULL, :], 0.0).then_inc(s_pad, 1)
                link = Chain(dve, s_ch)
                nc.vector.memset(eps[:, :], EPS)
                nc.vector.memset(ones[:, :], 1.0)
                nc.vector.memset(zeros[:, :], 0.0).then_inc(s_pad, 1)
                link(nc.vector.memset(dots_sb[:, :, :], 0.0))
                for c in range(FULL // XC):
                    dve.wait_ge(s_x[c], 16)
                    for t in range(c * XC, (c + 1) * XC):
                        nc.vector.bn_stats(stats[:, t % (2 * CHUNKS), :], acc[:, t, :])
                dve.wait_ge(s_x[4], 16)
                link(nc.vector.bn_stats(stats[:, FULL, :], acc[:, FULL, :]))
                row_statistics(link, nc, stats, ln, s_var)
                dve.wait_ge(s_std, 1)
                link(nc.vector.reciprocal(ln[:, 1, :], ln[:, 2, :]))
                base = link.n

                def row(t, slot):
                    dve.wait_ge(s_turn, t + 1)
                    nc.vector.tensor_scalar(work[:, slot, :], acc[:, bass.ds(t, 1), :], ln[:, 0, bass.ds(t, 1)],
                                            ln[:, 1, bass.ds(t, 1)], ALU.subtract, ALU.mult).then_inc(s_row, 1)
                over_tiles(dve, TILES, 2, row)

                for k in range(KD):
                    dve.wait_ge(s_kept, TILES + 2)
                    for c in range(CHUNKS):
                        last = nc.vector.bn_stats(stats[:, c, :], xnT[:, k, c * CH:(c + 1) * CH])
                    link(last)
                    link(nc.vector.bn_aggr(fm[:, k, 0:2], stats[:, 0:CHUNKS, :].rearrange("p c s -> p (c s)")))
                nc.vector.tensor_copy(fm[:, 0, 2:3], fm[:, 0, 1:2]).then_inc(s_var, 1)
                dve.wait_ge(s_std, 3)
                for k in range(KD):
                    link(nc.vector.tensor_scalar_add(fm[:, k, 2:3], fm[:, k, 3:4], 1e-4))
                    link(nc.vector.reciprocal(fm[:, k, 3:4], fm[:, k, 2:3]))

                dve.wait_ge(s_w, 16 * LOADS)
                heads = wkv[:, :, :].rearrange("p k (h c) -> p (k h) c", c=DH)
                hm = sq[:, 0, 0, 0:2 * 2 * HEADS]
                link(nc.vector.tensor_reduce(hm, heads, AX.X, ALU.add))
                link(nc.vector.tensor_scalar_mul(hm, hm, 1.0 / DH))
                link(nc.vector.tensor_tensor(heads, heads, hm.unsqueeze(2).to_broadcast([P, 4 * HEADS, DH]), ALU.subtract))
                link(nc.vector.tensor_tensor(brow[:, 2, :], brow[:, 0, :], brow[:, 1, :], ALU.add))

                dve.wait_ge(s_dst, 32)
                nc.vector.tensor_copy(src_tab, raw[1])
                link(nc.vector.tensor_copy(dst_tab, raw[0]))
                by_group = dst_tab.rearrange("p (g j) -> p g j", j=EPT)
                nc.vector.tensor_reduce(bounds[:, 0, :], by_group, AX.X, ALU.min)
                nc.vector.tensor_reduce(bounds[:, 1, :], by_group, AX.X, ALU.max).then_inc(s_var, 1)

            @block.scalar
            def _(act):
                act.wait_ge(s_var, 1)
                nc.scalar.activation(ln[:, 2, :], ln[:, 1, :], ACT.Sqrt, bias=eps[:, :]).then_inc(s_std, 1)

                def keep(t, slot):
                    act.wait_ge(s_turn, t + 3)
                    to = xnT[:, :, bass.ds(t * P, P)]
                    nc.scalar.copy(to, bank[slot][:, 0:D].rearrange("p (k n) -> p k n", k=KD)).then_inc(s_kept, 1)
                act.sem_inc(s_kept, 2)
                over_tiles(act, TILES, 2, keep)
                act.wait_ge(s_var, 2)
                for k in range(KD):
                    nc.scalar.activation(fm[:, k, 3:4], fm[:, k, 1:2], ACT.Sqrt, scale=N / (N - 1.0)).then_inc(s_std, 1)

            @block.tensor
            def _(pe):
                pe.wait_ge(s_const, 1)
                pe.sem_inc(s_turn, 2)

                def turn(t, slot):
                    pe.wait_ge(s_row, t + 1)
                    pe.wait_ge(s_kept, t + 1)
                    for k in range(KD):
                        last = nc.tensor.transpose(bank[slot][:, k * P:(k + 1) * P], work[:, slot, k * P:(k + 1) * P], ident[:, :])
                    last.then_inc(s_turn, 1)
                over_tiles(pe, TILES, 2, turn)

        b_ready = sem("b_operand_ready")
        b_done = sem("b_product_ready")
        b_copied = sem("b_product_copied")
        b_stored = [sem(f"b_rows_stored{i}") for i in range(2)]
        b_ch = sem("b_vector_chain")
        b_bt = sem("b_bounds_turned")
        b_bc = sem("b_bounds_columns")
        b_br = sem("b_bounds_rows")
        with nc.Block() as block:
            @block.vector
            def _(dve):
                def operand(t, slot):
                    dve.wait_ge(b_done, t + 1)
                    for k in range(KD):
                        last = nc.vector.tensor_scalar(ring[:, slot, k, :], xnT[:, k, bass.ds(t * P, P)], fm[:, k, 0:1],
                                                       fm[:, k, 3:4], ALU.subtract, ALU.mult)
                    last.then_inc(b_ready, 1)
                over_tiles(dve, TILES, 2, operand)

                link = Chain(dve, b_ch)
                dve.wait_ge(b_bt, 1)
                for b in range(2):
                    for m, op in ((0, ALU.min), (1, ALU.max)):
                        link(nc.vector.tensor_reduce(bcol[:, b, m:m + 1], bank[2 + b][0:GB, m * P:(m + 1) * P], AX.X, op))
                link(nc.vector.tensor_tensor(bcol_i[:, :, :], bcol[:, :, 1:2], bcol[:, :, 0:1], ALU.subtract))
                link(nc.vector.tensor_single_scalar(bcol_i[:, :, :], bcol_i[:, :, :], 7, ALU.arith_shift_right))
                nc.vector.tensor_copy(bcol[:, :, 1:2], bcol_i[:, :, :]).then_inc(b_bc, 1)
                dve.wait_ge(b_br, 1)
                nc.vector.tensor_copy(table[:, 0:GROUPS], bank[4][0:1, 0:GROUPS])
                nc.vector.tensor_reduce(table[:, GROUPS:], bank[4][0:1, 256:256 + GROUPS], AX.X, ALU.max)
                by_group = dst_tab.rearrange("p (g j) -> p g j", j=EPT)
                link(nc.vector.tensor_tensor(by_group, by_group, bank[6][:, 0:GROUPS].unsqueeze(2).to_broadcast([P, GROUPS, EPT]),
                                             ALU.subtract))

            @block.tensor
            def _(pe):
                pe.sem_inc(b_done, 2)

                def product(t, slot):
                    pe.wait_ge(b_ready, t + 1)
                    pe.wait_ge(b_copied, t + 1)
                    for k in range(KD):
                        last = nc.tensor.matmul(bank[slot][:, 0:D], ring[:, slot, k, :], wg[:, k, :], start=k == 0, stop=k == KD - 1)
                    last.then_inc(b_done, 1)
                over_tiles(pe, TILES, 2, product)

                for b in range(2):
                    for m in range(2):
                        last = nc.tensor.transpose(bank[2 + b][0:GB, m * P:(m + 1) * P], bounds[:, m, b * GB:(b + 1) * GB], ident[:, :])
                last.then_inc(b_bt, 1)
                pe.wait_ge(b_bc, 1)
                for m in range(2):
                    for b in range(2):
                        nc.tensor.matmul(bank[4][0:1, m * 256 + b * GB:m * 256 + (b + 1) * GB], bcol[:, b, m:m + 1],
                                         ident[0:GB, 0:GB], start=True, stop=True)
                for b in range(2):
                    last = nc.tensor.matmul(bank[6][:, b * GB:(b + 1) * GB], bcol[:, b, 0:1].to_broadcast([GB, P]),
                                            ident[0:GB, 0:GB], start=True, stop=True)
                last.then_inc(b_br, 1)

            @block.scalar
            def _(act):
                act.sem_inc(b_copied, 2)

                act.sem_inc(b_stored[0], 16)
                act.sem_inc(b_stored[1], 16)

                def rows(t, slot, turn):
                    act.wait_ge(b_done, t + 3)
                    act.wait_ge(b_stored[slot], turn * 16 + 16)
                    nc.scalar.copy(work[:, slot, :], bank[slot][:, 0:D]).then_inc(b_copied, 1)
                with act.Fori(0, TILES // 2) as i:
                    for u in range(2):
                        rows(i * 2 + u, u, i)
                rows(TILES - 1, 0, TILES // 2)

            @block.sync
            def _(sp):
                def store(t, slot):
                    sp.wait_ge(b_copied, t + 3)
                    sp.dma_start(feat_rows[bass.ds(t * P, P), :], work[:, slot, :]).then_inc(b_stored[slot], 16)
                over_tiles(sp, TILES, 2, store)
                sp.wait_ge(s_zero, 16 * (SUMS + 1))
                sp.wait_ge(b_stored[0], 16 * (TILES // 2 + 2))
                sp.wait_ge(b_stored[1], 16 * (TILES // 2 + 1))

        edge_phase(
            nc, sem, acc=acc, xnT=xnT, src_tab=src_tab, dst_tab=dst_tab, ew_tab=ew_tab, msg=msg, src_row=src_row, same=same,
            onehot=onehot, joined=joined, window=window,
            earlier=earlier, spare=spare, clash=clash, unused=unused, target=target, src_rows=src_rows, wkv=wkv, wq=wq, woT=woT, iota=iota, ones=ones, eps=eps, zeros=zeros, brow=brow,
            ring=ring, sq=sq, k_sb=k_sb, v_sb=v_sb, hs=hs, table=table, dots_sb=dots_sb, pq_sb=pq_sb, mix=mix,
            tiny=tiny, bank=bank, feat_rows=feat_rows, edge_sums=edge_sums, big=edge_area)
        expert_phase(
            nc, sem, acc=acc, yT=xnT, w1=w1, w2=w2, w1_sb=w1_sb, w2_sb=w2_sb, wr=wr, b1_sb=b1_sb, b2_sb=b2_sb, ident=ident,
            eps=eps, work=work, ring=ring, stats=stats, ln=ln, router=router, route1=route1, rank=rank, combT=combT,
            comb1=comb1, bank=bank, out=out, hbuf=onehot)


def row_statistics(link, nc, stats, ln, signal):
    even, odd = stats[:, 0:TILES, 1], stats[:, 0:TILES, 4]
    link(nc.vector.tensor_tensor(ln[:, 0, :], even, odd, ALU.add))
    link(nc.vector.tensor_tensor(ln[:, 3, :], even, odd, ALU.subtract))
    link(nc.vector.tensor_scalar_mul(ln[:, 0, :], ln[:, 0, :], 0.5))
    link(nc.vector.tensor_tensor(ln[:, 4, :], stats[:, 0:TILES, 2], stats[:, 0:TILES, 5], ALU.add))
    link(nc.vector.tensor_tensor(ln[:, 3, :], ln[:, 3, :], ln[:, 3, :], ALU.mult))
    link(nc.vector.tensor_scalar_mul(ln[:, 4, :], ln[:, 4, :], 1.0 / D))
    nc.vector.scalar_tensor_tensor(out=ln[:, 1, :], in0=ln[:, 3, :], scalar=0.25, in1=ln[:, 4, :], op0=ALU.mult,
                                   op1=ALU.add).then_inc(signal, 1)


def edge_phase(nc, sem, *, acc, xnT, src_tab, dst_tab, ew_tab, msg, src_row, same, onehot, joined, window,
               earlier, spare, clash, unused, target, src_rows, wkv, wq, woT,
               iota, ones, eps, zeros, brow, ring, sq, k_sb, v_sb, hs, table, dots_sb, pq_sb, mix, tiny, bank,
               feat_rows, edge_sums, big):
    jbank, mbank = bank[0], [bank[1], bank[2]]
    kb, vb, dots, mm = bank[3], bank[4], bank[5], bank[6]
    QPI = 4
    ITERS = QUADS // QPI

    rows_in = [sem(f"c_sources_loaded{i}") for i in range(2)]
    win_in = [sem(f"c_window_loaded{i}") for i in range(2)]
    same_made = sem("c_same_made")
    built = sem("c_matrices_built")
    idx_ch = sem("c_index_chain")
    j_done = sem("c_joined_ready")
    j_kept = sem("c_joined_kept")
    m_done = sem("c_messages_ready")
    m_kept = sem("c_messages_kept")
    scattered = [sem(f"c_scattered{r}") for r in range(SUMS)]
    shifted = sem("c_windows_shifted")
    aimed = sem("c_targets_ready")
    ring_ready = sem("c_ring_ready")
    kv_done = sem("c_kv_ready")
    sq_done = sem("c_squares_ready")
    k_kept = sem("c_k_kept")
    ss_done = sem("c_square_sums_ready")
    sd_done = sem("c_deviations_ready")
    c_ch = sem("c_vector_chain")
    v_ready = sem("c_v_ready")
    dots_done = sem("c_dots_added")
    dots_kept = sem("c_dots_kept")
    p_done = sem("c_p_ready")
    p_kept = sem("c_p_kept")
    mix_done = sem("c_mix_ready")
    mix_kept = sem("c_mix_kept")
    mm_done = sem("c_mixed_ready")
    mm_added = sem("c_mixed_added")
    act_waits = sem("c_act_waits_passed")
    sp_waits = sem("c_sync_waits_passed")


    def slot_free(eng, v, u):
        if not isinstance(v, int) or v:
            for j in range(QT):
                eng.wait_ge(scattered[u % 2 * QT + j], (v * 2 + u // 2 - 1) * 16)

    def back(v, u):
        return (v, u - 1) if u else (v - 1, QPI - 1)

    def further_passes(eng, one):
        passes = eng.value_load(table[0:1, GROUPS:GROUPS + 1], min_val=0, max_val=TILES)
        with eng.If(0 < passes):
            with eng.Fori(1, passes + 1) as w:
                one(w, w * ITERS)

    with nc.Block() as block:
        @block.sync
        def _(sp):
            def load(v, i, h):
                sp.wait_ge(built, v * QPI + h * 2 + 2)
                sp.sem_inc(sp_waits, 1)
                row = src_rows[bass.ds((i * 2 + h) * GE, GE)].unsqueeze(0).to_broadcast([P, GE])
                sp.dma_start(src_row[:, 2 * h:2 * h + 2, :, :].rearrange("p u j e -> p (u j e)"), row).then_inc(rows_in[h], 16)
                sp.wait_ge(m_done, (v * 2 + h) * 4 + 4)
                sp.sem_inc(sp_waits, 1)
                start = sp.value_load(table[0:1, bass.ds(i * 2 + h, 1)], min_val=0, max_val=N - 1)
                sp.dma_start(window[:, h, :], feat_rows[bass.ds(start, P), :]).then_inc(win_in[h], 16)

            with sp.Fori(0, ITERS) as i:
                load(i, i, 0)
                load(i, i, 1)

            def again(w, v):
                sp.wait_ge(shifted, w)
                sp.sem_inc(sp_waits, 1)
                with sp.Fori(0, ITERS) as i:
                    load(v + i, i, 0)
                    load(v + i, i, 1)
            further_passes(sp, again)

        @block.gpsimd
        def _(pool):
            def scatter(v, u):
                pool.wait_ge(m_kept, (v * QPI + u) * 2 + 4)
                pool.sem_inc(pool_waits, 1)
                pool.wait_ge(aimed, v * QPI + u + 1)
                pool.sem_inc(pool_waits, 1)
                for j in range(QT):
                    r = u % 2 * QT + j
                    if not isinstance(v, int) or u >= 2:
                        pool.wait_ge(scattered[r], (v * 2 + u // 2) * 16)
                        pool.sem_inc(pool_waits, 1)
                    nc.gpsimd.indirect_dma_start(
                        out=edge_sums[r], out_offset=bass.IndirectOffsetOnAxis(ap=target[:, u, j:j + 1], axis=0),
                        in_=msg[:, u, j, :], in_offset=None, compute_op=ALU.add).then_inc(scattered[r], 16)
            pool_waits = sem("c_pool_waits_passed")
            for u in range(QPI):
                scatter(0, u)
            with pool.Fori(1, ITERS) as i:
                for u in range(QPI):
                    scatter(i, u)

            def again(w, v):
                with pool.Fori(0, ITERS) as i:
                    for u in range(QPI):
                        scatter(v + i, u)
                for r in range(SUMS):
                    pool.wait_ge(scattered[r], (v + ITERS) * 32)
                    pool.sem_inc(pool_waits, 1)
            for r in range(SUMS):
                pool.wait_ge(scattered[r], ITERS * 32)
                pool.sem_inc(pool_waits, 1)
            further_passes(pool, again)

        @block.tensor
        def _(pe):
            pe.sem_inc(m_done, 8)
            pe.sem_inc(j_done, 2)

            def join(v, u):
                q = v * QPI + u
                pe.wait_ge(built, q + 5)
                pe.wait_ge(j_kept, q + 1)
                for j in range(QT):
                    last = nc.tensor.matmul(jbank[:, j * P:(j + 1) * P], onehot[:, u % 2, j, :], same[:, u, j, :],
                                            start=True, stop=True)
                last.then_inc(j_done, 1)

            def messages(v, u):
                q = v * QPI + u
                pe.wait_ge(win_in[u // 2], v * 16 + 16)
                pe.wait_ge(j_kept, q + 2)
                for b in range(2):
                    pe.wait_ge(m_kept, q * 2 + b + 1)
                    for j in range(2):
                        last = nc.tensor.matmul(mbank[b][:, j * D:(j + 1) * D], joined[:, u % 2, 2 * b + j, :],
                                                window[:, u // 2, :], start=True, stop=True)
                    last.then_inc(m_done, 1)

            def attend(i):
                pe.wait_ge(ring_ready, i + 1)
                pe.wait_ge(k_kept, i + 1)
                pe.wait_ge(v_ready, i + 1)
                for c, b in ((0, kb), (1, vb)):
                    for k in range(KD):
                        last = nc.tensor.matmul(b[:, :], ring[:, 0, k, :], wkv[:, k, c * INNER:(c + 1) * INNER],
                                                start=k == 0, stop=k == KD - 1)
                last.then_inc(kv_done, 1)

            def dot(i):
                pe.wait_ge(v_ready, i + 2)
                pe.wait_ge(k_kept, i + 2)
                for q in range(PAIRS):
                    last = nc.tensor.matmul(dots[:, q * P:(q + 1) * P], v_sb[:, 2 * q:2 * q + 2, :].rearrange("p h c -> p (h c)"),
                                            k_sb[:, q * P:(q + 1) * P], start=False, stop=False, skip_group_check=True)
                last.then_inc(dots_done, 1)

            def mixed(i):
                pe.wait_ge(ring_ready, i + 1)
                pe.wait_ge(mm_added, i + 1 - TILES)
                for k in range(KD):
                    nc.tensor.matmul(mm[:, 0:D], ring[:, 0, k, :], mix[:, k, :], start=k == 0, stop=False)
                nc.tensor.matmul(mm[:, 0:D], ones[0:1, :], brow[0:1, 2, :], start=False, stop=True).then_inc(mm_done, 1)

            def step(v, first=False, before=None, after=None):
                if before:
                    before(v)
                for u in range(QPI):
                    join(v, u)
                    if u or not first:
                        messages(*back(v, u))
                if after:
                    after(v)

            nc.tensor.matmul(dots[:, :], zeros[:, 0:P], wkv[:, 0, 0:512], start=True, stop=False, skip_group_check=True)
            step(0, True, attend, dot)
            with pe.Fori(1, TILES) as i:
                step(i, False, attend, dot)
            nc.tensor.matmul(dots[:, :], zeros[:, 0:P], wkv[:, 0, 0:512], start=False, stop=True,
                             skip_group_check=True).then_inc(dots_done, 1)

            pe.wait_ge(dots_kept, 1)
            for q in range(PAIRS):
                b = (kb, vb)[q % 2]
                if q >= 2:
                    pe.wait_ge(p_kept, q - 1)
                nc.tensor.matmul(b[:, 0:D], dots_sb[:, q, :], woT[:, q, :], start=True, stop=True).then_inc(p_done, 1)
            pe.wait_ge(p_kept, PAIRS)
            for k in range(KD):
                for q in range(PAIRS):
                    last = nc.tensor.matmul(mm[:, k * D:(k + 1) * D], wq[:, q, k * P:(k + 1) * P], pq_sb[:, q, :],
                                            start=q == 0, stop=q == PAIRS - 1)
            last.then_inc(mix_done, 1)
            pe.wait_ge(mix_kept, 1)
            with pe.Fori(TILES, 2 * TILES) as i:
                step(i, False, mixed)
            with pe.Fori(2 * TILES, ITERS) as i:
                step(i)
            messages(ITERS - 1, QPI - 1)

            def again(w, v):
                step(v, True)
                with pe.Fori(1, ITERS) as i:
                    step(v + i)
                messages(v + (ITERS - 1), QPI - 1)
            further_passes(pe, again)

        @block.scalar
        def _(act):
            act.sem_inc(k_kept, 1)
            act.sem_inc(j_kept, 1)
            act.sem_inc(m_kept, 2)

            def keep_joined(v, u):
                q = v * QPI + u
                act.wait_ge(j_done, q + 3)
                nc.scalar.copy(joined[:, u % 2, :, :].rearrange("p j e -> p (j e)"), jbank[:, :]).then_inc(j_kept, 1)

            def rows(v, u):
                q = v * QPI + u
                slot_free(act, v, u)
                for b in range(2):
                    act.wait_ge(m_done, q * 2 + b + 9)
                    nc.scalar.copy(msg[:, u, 2 * b:2 * b + 2, :].rearrange("p j d -> p (j d)"), mbank[b][:, :]).then_inc(m_kept, 1)

            def keys(i):
                act.wait_ge(kv_done, i + 1)
                nc.scalar.activation(sq[:, 0, :, :].rearrange("p h c -> p (h c)"), kb[:, :], ACT.Square)
                nc.scalar.activation(sq[:, 1, :, :].rearrange("p h c -> p (h c)"), vb[:, :], ACT.Square).then_inc(sq_done, 1)
                act.wait_ge(dots_done, i + 1)
                nc.scalar.copy(k_sb[:, :], kb[:, :]).then_inc(k_kept, 1)

            def deviations(i):
                act.wait_ge(ss_done, i + 1)
                nc.scalar.activation(hs[:, 1, :], hs[:, 0, :], ACT.Sqrt, bias=eps[:, :], scale=1.0 / DH).then_inc(sd_done, 1)

            def operand(t):
                nc.scalar.copy(ring[:, 0, :, :], xnT[:, :, bass.ds(t * P, P)]).then_inc(ring_ready, 1)

            def attention(i, u):
                if u == 0:
                    keys(i)
                    operand(i + 1)
                if u == 1:
                    deviations(i)

            def mixing(i, u):
                if u == 0:
                    act.wait_ge(mm_done, i + 1 - TILES)
                    act.sem_inc(act_waits, 1)
                    operand(i + 1 - TILES)

            def step(v, first=False, other=None):
                for u in range(QPI):
                    keep_joined(v, u)
                    if u or not first:
                        rows(*back(v, u))
                    if other:
                        other(v, u)

            def last_attention(i, u):
                if u == 0:
                    keys(i)
                if u == 1:
                    deviations(i)

            operand(0)
            step(0, True, attention)
            with act.Fori(1, TILES - 1) as i:
                step(i, False, attention)
            step(TILES - 1, False, last_attention)
            for q in range(PAIRS):
                act.wait_ge(p_done, q + 1)
                nc.scalar.copy(pq_sb[:, q, :], (kb, vb)[q % 2][:, 0:D]).then_inc(p_kept, 1)
            act.wait_ge(mix_done, 1)
            nc.scalar.copy(mix[:, :, :], mm[:, :].rearrange("p (k d) -> p k d", k=KD)).then_inc(mix_kept, 1)
            operand(0)
            with act.Fori(TILES, 2 * TILES - 1) as i:
                step(i, False, mixing)
            with act.Fori(2 * TILES - 1, ITERS) as i:
                step(i)
            rows(ITERS - 1, QPI - 1)

            def again(w, v):
                step(v, True)
                with act.Fori(1, ITERS) as i:
                    step(v + i)
                rows(v + (ITERS - 1), QPI - 1)
            further_passes(act, again)

        @block.vector
        def _(dve):
            dve.sem_inc(built, 4)
            dve.sem_inc(v_ready, 1)
            dve.sem_inc(dots_done, 1)
            dve.sem_inc(mm_added, 1)

            def build(v, i, u):
                q = v * QPI + u
                at = i * (QPI * QT) + u * QT
                if u % 2 == 0:
                    dve.wait_ge(rows_in[u // 2], v * 16 + 16)
                for j in range(QT):
                    last = nc.vector.tensor_scalar(same[:, u, j, :], src_row[:, u, j, :],
                                                   src_tab[:, bass.ds(at + j, 1)], None, ALU.is_equal)
                last.then_inc(same_made, 1)
                dve.wait_ge(j_done, q + 1)
                for j in range(QT):
                    last = nc.vector.tensor_scalar(onehot[:, u % 2, j, :], iota[:, :], dst_tab[:, bass.ds(at + j, 1)],
                                                   ew_tab[:, bass.ds(at + j, 1)], ALU.is_equal, ALU.mult)
                last.then_inc(built, 1)

            def targets(v, i, u):
                q = v * QPI + u
                dve.wait_ge(same_made, q + 1)
                slot_free(dve, v, u)
                link = Chain(dve, idx_ch, q * 3)
                clashes, hit, off = (clash[:, u, n, :] for n in range(3))
                for j in range(QT):
                    last = nc.vector.tensor_tensor_reduce(out=unused[:, j, :], in0=same[:, u, j, :], in1=earlier[:, :],
                                                          scale=1.0, scalar=0.0, op0=ALU.mult, op1=ALU.add,
                                                          accum_out=clashes[:, j:j + 1])
                link(last)
                link(nc.vector.tensor_scalar_min(hit, clashes, 1.0))
                sources = src_tab[:, bass.ds(i * (QPI * QT) + u * QT, QT)]
                link(nc.vector.scalar_tensor_tensor(out=off, in0=sources, scalar=spare[:, :], in1=hit,
                                                    op0=ALU.subtract, op1=ALU.mult))
                nc.vector.tensor_tensor(target[:, u, :], sources, off, ALU.subtract).then_inc(aimed, 1)

            def values(i, u):
                if u == 1:
                    dve.wait_ge(sq_done, i + 1)
                    nc.vector.tensor_reduce(hs[:, 0, :], sq[:, :, :, :].rearrange("p a h c -> p (a h) c"), AX.X,
                                            ALU.add).then_inc(ss_done, 1)
                if u == 2:
                    link = Chain(dve, c_ch, i * 2)
                    dve.wait_ge(sd_done, i + 1)
                    link(nc.vector.reciprocal(hs[:, 2, :], hs[:, 1, :]))
                    link(nc.vector.tensor_tensor(hs[:, 2, 0:HEADS], hs[:, 2, 0:HEADS], hs[:, 2, HEADS:], ALU.mult))
                    dve.wait_ge(dots_done, i + 1)
                    nc.vector.tensor_tensor(v_sb[:, :, :], vb[:, :].rearrange("p (h c) -> p h c", h=HEADS),
                                            hs[:, 2, 0:HEADS].unsqueeze(2).to_broadcast([P, HEADS, DH]), ALU.mult).then_inc(v_ready, 1)

            def mixed(i, u):
                if u == 1:
                    dve.wait_ge(mm_done, i + 1 - TILES)
                    to = acc[:, bass.ds(i - TILES, 1), :].rearrange("p t d -> p (t d)")
                    nc.vector.tensor_tensor(to, to, mm[:, 0:D], ALU.add).then_inc(mm_added, 1)

            def step(v, i, first=False, other=None):
                for u in range(QPI):
                    build(v, i, u)
                    if u or not first:
                        targets(*back(v, u)[:1], *back(i, u))
                    if other:
                        other(v, u)

            step(0, 0, True, values)
            with dve.Fori(1, TILES) as i:
                step(i, i, False, values)
            dve.wait_ge(dots_done, TILES + 2)
            for h in range(2):
                blk = dots_sb[h * DH:(h + 1) * DH, :, h * DH:(h + 1) * DH]
                last = nc.vector.tensor_scalar_mul(blk, dots[h * DH:(h + 1) * DH, :].rearrange("p (q d) -> p q d", q=PAIRS)[
                    :, :, h * DH:(h + 1) * DH], 1.0 / N)
            last.then_inc(dots_kept, 1)
            with dve.Fori(TILES, 2 * TILES) as i:
                step(i, i, False, mixed)
            with dve.Fori(2 * TILES, ITERS) as i:
                step(i, i)
            targets(ITERS - 1, ITERS - 1, QPI - 1)

            def again(w, v):
                dve.wait_ge(built, v * QPI + 4)
                nc.vector.tensor_scalar_add(dst_tab, dst_tab, -float(P))
                nc.vector.tensor_scalar(table[:, 0:GROUPS], table[:, 0:GROUPS], float(P), N - 1.0, ALU.add, ALU.min
                                        ).then_inc(shifted, 1)
                dve.wait_ge(shifted, w)
                step(v, 0, True)
                with dve.Fori(1, ITERS) as i:
                    step(v + i, i)
                targets(v + (ITERS - 1), ITERS - 1, QPI - 1)
            further_passes(dve, again)

    CT = 7
    SLOTS = 4
    loaded = [sem(f"d_sum_loaded{r}") for r in range(SUMS)]
    used = sem("d_sum_added")
    parts = [big[:, r * CT * D:(r + 1) * CT * D].rearrange("p (t d) -> p t d", t=CT) for r in range(SLOTS)]
    with nc.Block() as block:
        @block.sync
        def _(sp):
            with sp.Fori(0, TILES // CT) as c:
                for r in range(SUMS):
                    sp.wait_ge(used, c * SUMS + r + 1)
                    sp.dma_start(parts[r % SLOTS], edge_sums[r][bass.ds(c * (CT * P), CT * P), :].rearrange("(t p) d -> p t d", p=P)
                                 ).then_inc(loaded[r], 16)

        @block.vector
        def _(dve):
            dve.sem_inc(used, SLOTS)
            with dve.Fori(0, TILES // CT) as c:
                for r in range(SUMS):
                    dve.wait_ge(loaded[r], c * 16 + 16)
                    dve.wait_ge(used, c * SUMS + r + SLOTS)
                    to = acc[:, bass.ds(c * CT, CT), :]
                    nc.vector.tensor_tensor(to, to, parts[r % SLOTS], ALU.add).then_inc(used, 1)


def expert_phase(nc, sem, *, acc, yT, w1, w2, w1_sb, w2_sb, wr, b1_sb, b2_sb, ident, eps, work, ring, stats, ln,
                 router, route1, rank, combT, comb1, bank, out, hbuf):
    w_in = sem("e_expert_weights_loaded")
    ch = sem("e_vector_chain")
    var = sem("e_variance_ready")
    std = sem("e_deviation_ready")
    row = sem("e_row_ready")
    turned = sem("e_row_turned")
    kept = sem("e_row_kept")
    ringed = sem("e_operand_ready")
    logit = sem("e_logits_ready")
    logit_kept = sem("e_logits_kept")
    shifted = sem("e_logits_shifted")
    exped = sem("e_exponentials_ready")
    probs, one1, one2, tmp, comb = (router[:, i, :, :] for i in range(5))
    top, top2, den, inv = (route1[:, i, :] for i in range(4))

    def wide(a):
        return a.unsqueeze(2).to_broadcast([P, TILES, EXPERTS])

    with nc.Block() as block:
        @block.sync
        def _(sp):
            sp.dma_start(w1_sb, w1.rearrange("e (k p) n -> p e k n", p=P)).then_inc(w_in, 16)
            sp.dma_start(w2_sb, w2.rearrange("e (k p) n -> p e k n", p=P)).then_inc(w_in, 16)
            sp.wait_ge(w_in, 32)

        @block.vector
        def _(dve):
            link = Chain(dve, ch)
            for t in range(TILES):
                last = nc.vector.bn_stats(stats[:, t, :], acc[:, t, :])
            link(last)
            row_statistics(link, nc, stats, ln, var)
            dve.wait_ge(std, 1)
            link(nc.vector.reciprocal(ln[:, 1, :], ln[:, 2, :]))

            def logits(t, slot):
                dve.wait_ge(logit, t + 1)
                nc.vector.tensor_copy(router[:, 0, bass.ds(t, 1), :].rearrange("p t e -> p (t e)"),
                                      bank[2 + slot][:, 0:EXPERTS]).then_inc(logit_kept, 1)

            def step(t, slot):
                dve.wait_ge(turned, t + 1)
                src = acc[:, bass.ds(t, 1), :].rearrange("p t d -> p (t d)")
                nc.vector.tensor_scalar(work[:, slot, :], src, ln[:, 0, bass.ds(t, 1)], ln[:, 1, bass.ds(t, 1)],
                                        ALU.subtract, ALU.mult).then_inc(row, 1)

            def keep(t, slot):
                dve.wait_ge(turned, t + 3)
                dve.wait_ge(kept, t + 1)
                nc.vector.tensor_copy(ring[:, slot, :, :], bank[slot][:, 0:D].rearrange("p (k n) -> p k n", k=KD)
                                      ).then_inc(ringed, 1)
                src = acc[:, bass.ds(t, 1), :].rearrange("p t d -> p (t d)")
                nc.vector.tensor_tensor(src, src, work[:, slot, :], ALU.add)
            dve.sem_inc(logit_kept, 2)

            def both(t, slot):
                step(t, slot)
                keep(t, slot)
                logits(t, slot)
            over_tiles(dve, TILES, 2, both)

            dve.wait_ge(logit_kept, TILES + 2)
            link(nc.vector.tensor_reduce(top, probs, AX.X, ALU.max))
            nc.vector.tensor_tensor(tmp, probs, wide(top), ALU.subtract).then_inc(shifted, 1)
            dve.wait_ge(exped, 1)
            link(nc.vector.tensor_reduce(den, comb, AX.X, ALU.add))
            link(nc.vector.reciprocal(inv, den))
            link(nc.vector.tensor_tensor(probs, comb, wide(inv), ALU.mult))
            by_rank = rank[:, :].unsqueeze(1).to_broadcast([P, TILES, EXPERTS])
            for n, (best, one) in enumerate(((top, one1), (top2, one2))):
                of = probs if n == 0 else comb
                link(nc.vector.tensor_reduce(best, of, AX.X, ALU.max))
                link(nc.vector.tensor_tensor(tmp, of, wide(best), ALU.is_equal))
                link(nc.vector.tensor_tensor(tmp, tmp, by_rank, ALU.mult))
                link(nc.vector.tensor_reduce(den, tmp, AX.X, ALU.max))
                link(nc.vector.tensor_tensor(one, tmp, wide(den), ALU.is_equal))
                if n == 0:
                    link(nc.vector.scalar_tensor_tensor(out=comb, in0=one, scalar=-2.0, in1=probs, op0=ALU.mult, op1=ALU.add))
            link(nc.vector.tensor_tensor(den, top, top2, ALU.add))
            link(nc.vector.tensor_scalar_max(den, den, 1e-12))
            link(nc.vector.reciprocal(inv, den))
            link(nc.vector.tensor_tensor(tmp, one1, one2, ALU.add))
            link(nc.vector.tensor_tensor(tmp, tmp, probs, ALU.mult))
            link(nc.vector.tensor_tensor(comb, tmp, wide(inv), ALU.mult))

        @block.tensor
        def _(pe):
            pe.sem_inc(turned, 2)

            def turn(t, slot):
                pe.wait_ge(row, t + 1)
                pe.wait_ge(ringed, t + 1)
                for k in range(KD):
                    last = nc.tensor.transpose(bank[slot][:, k * P:(k + 1) * P], work[:, slot, k * P:(k + 1) * P], ident[:, :])
                last.then_inc(turned, 1)

                pe.wait_ge(ringed, t + 3)
                pe.wait_ge(logit_kept, t + 1)
                for k in range(KD):
                    last = nc.tensor.matmul(bank[2 + slot][:, 0:EXPERTS], ring[:, slot, k, :], wr[:, k, :],
                                            start=k == 0, stop=k == KD - 1)
                last.then_inc(logit, 1)
            pe.sem_inc(ringed, 2)
            over_tiles(pe, TILES, 2, turn)

        @block.scalar
        def _(act):
            act.wait_ge(var, 1)
            nc.scalar.activation(ln[:, 2, :], ln[:, 1, :], ACT.Sqrt, bias=eps[:, :]).then_inc(std, 1)
            act.sem_inc(kept, 2)

            def keep(t, slot):
                act.wait_ge(ringed, t + 3)
                nc.scalar.copy(yT[:, :, bass.ds(t * P, P)], ring[:, slot, :, :]).then_inc(kept, 1)
            over_tiles(act, TILES, 2, keep)
            act.wait_ge(shifted, 1)
            nc.scalar.activation(comb, tmp, ACT.Exp).then_inc(exped, 1)

    c_staged = sem("f_weights_staged")
    c_turned = sem("f_weights_turned")
    c_kept = sem("f_weights_kept")
    l1_done = sem("f_hidden_ready")
    gelued = sem("f_gelu_ready")
    l2_done = sem("f_output_ready")
    added = sem("f_output_added")
    b_done = sem("f_bias_ready")
    bias_added = sem("f_bias_added")
    stored = sem("f_stored")
    dve_waits = sem("f_vector_waits_passed")
    hp = [bank[0], bank[1]]
    op = [bank[2], bank[3]]
    ctb, bb = bank[4], bank[5]
    hidden = [hbuf[:, s, 0:KD, :] for s in range(2)]
    with nc.Block() as block:
        @block.tensor
        def _(pe):
            def layer1(t, e):
                n = t * EXPERTS + e
                pe.wait_ge(gelued, n + 1)
                for h in range(KD):
                    for k in range(KD):
                        last = nc.tensor.matmul(hp[e % 2][:, h * P:(h + 1) * P], w1_sb[:, e, k, h * P:(h + 1) * P],
                                                yT[:, k, bass.ds(t * P, P)], start=k == 0, stop=k == KD - 1)
                last.then_inc(l1_done, 1)

            def layer2(t, e):
                n = t * EXPERTS + e
                pe.wait_ge(gelued, n + 3)
                pe.wait_ge(added, n + 1)
                for k in range(KD):
                    last = nc.tensor.matmul(op[e % 2][:, 0:D], hidden[e % 2][:, k, :], w2_sb[:, e, k, :], start=k == 0, stop=k == KD - 1)
                last.then_inc(l2_done, 1)

            def biases(t):
                pe.wait_ge(c_staged, t + 1)
                nc.tensor.transpose(ctb[0:EXPERTS, 0:P], comb1[:, :], ident[:, :]).then_inc(c_turned, 1)

            def biases2(t):
                pe.wait_ge(c_kept, t + 1)
                nc.tensor.matmul(bb[:, 0:D], combT[:, :], b2_sb[:, :], start=True, stop=True).then_inc(b_done, 1)

            def tile(t, more):
                biases(t)
                for e in range(EXPERTS):
                    if e + 1 < EXPERTS:
                        layer1(t, e + 1)
                    elif more:
                        layer1(t + 1, 0)
                    if e == 2:
                        biases2(t)
                    layer2(t, e)
            layer1(0, 0)
            with pe.Fori(0, TILES - 1) as t:
                tile(t, True)
            tile(TILES - 1, False)

        @block.scalar
        def _(act):
            act.sem_inc(gelued, 2)
            act.sem_inc(l2_done, 2)
            with act.Fori(0, TILES) as t:
                for e in range(EXPERTS):
                    n = t * EXPERTS + e
                    act.wait_ge(l1_done, n + 1)
                    act.wait_ge(l2_done, n + 1)
                    for h in range(KD):
                        last = nc.scalar.activation(hidden[e % 2][:, h, :], hp[e % 2][:, h * P:(h + 1) * P], ACT.Gelu,
                                                    bias=b1_sb[:, e, h:h + 1])
                    last.then_inc(gelued, 1)

        @block.vector
        def _(dve):
            dve.sem_inc(added, 2)

            def tile(t, slot):
                nc.vector.tensor_copy(comb1[:, :], router[:, 4, bass.ds(t, 1), :].rearrange("p t e -> p (t e)")
                                      ).then_inc(c_staged, 1)
                dve.wait_ge(c_turned, t + 1)
                nc.vector.tensor_copy(combT[:, :], ctb[0:EXPERTS, 0:P]).then_inc(c_kept, 1)
                to = acc[:, bass.ds(t, 1), :].rearrange("p t d -> p (t d)")
                last = None
                for e in range(EXPERTS):
                    n = t * EXPERTS + e
                    dve.wait_ge(added, n + 2)
                    if e == 4:
                        dve.wait_ge(b_done, t + 1)
                        nc.vector.tensor_tensor(to, to, bb[:, 0:D], ALU.add).then_inc(bias_added, 1)
                        dve.wait_ge(bias_added, t + 1)
                    dve.wait_ge(l2_done, n + 3)
                    last = nc.vector.scalar_tensor_tensor(out=to, in0=op[e % 2][:, 0:D],
                                                          scalar=router[:, 4, bass.ds(t, 1), e:e + 1].rearrange("p t e -> p (t e)"),
                                                          in1=to, op0=ALU.mult, op1=ALU.add)
                    last.then_inc(added, 1)
            over_tiles(dve, TILES, 1, tile)

        @block.sync
        def _(sp):
            with sp.Fori(0, FULL) as t:
                sp.wait_ge(added, t * EXPERTS + EXPERTS + 2)
                sp.dma_start(out[bass.ds(t * P, P), :], acc[:, bass.ds(t, 1), :].rearrange("p t d -> p (t d)")).then_inc(stored, 16)
            sp.wait_ge(added, TILES * EXPERTS + 2)
            sp.dma_start(out[FULL * P:N, :], acc[0:LAST, FULL, :]).then_inc(stored, 16)
            sp.wait_ge(stored, 16 * TILES)


def kernel(**inputs):
    import numpy as np
    import concourse.bacc as bacc
    from concourse.bass_utils import run_bass_kernel_spmd

    def a(name):
        return np.ascontiguousarray(inputs[name])

    def grouped(v):
        return np.concatenate([v[:(GROUPS - 1) * GE], v[EDGES - GE:]])

    def by_partition(v):
        return np.ascontiguousarray(grouped(v).reshape(COLS, P).T)

    qkv = a("L0_mix_w_qkv")
    arrays = {
        "x": a("x"), "src": by_partition(a("src")), "dst": by_partition(a("dst")), "ew": by_partition(a("edge_weight")),
        "src_rows": grouped(a("src")),
        "w_gnn": a("L0_gnn_weight"), "b_gnn": a("L0_gnn_bias").reshape(1, D),
        "w_kvT": np.ascontiguousarray(qkv[INNER:].T), "w_q": np.ascontiguousarray(qkv[:INNER]),
        "w_outT": np.ascontiguousarray(a("L0_mix_w_out").T), "b_out": a("L0_mix_b_out").reshape(1, D),
        "w_routerT": np.ascontiguousarray(a("L0_ffn_router_w").T), "w1": a("L0_ffn_w1"),
        "b1T": np.ascontiguousarray(a("L0_ffn_b1").reshape(EXPERTS, KD, P).transpose(2, 0, 1)), "w2": a("L0_ffn_w2"), "b2": a("L0_ffn_b2"),
    }
    nc = bacc.Bacc("TRN2", target_bir_lowering=False, num_devices=1)
    args = [nc.dram_tensor(f"in_{n}", v.shape, mybir.dt.from_np(v.dtype), kind="ExternalInput").ap() for n, v in arrays.items()]
    out = nc.dram_tensor("out_0", (N, D), F32, kind="ExternalOutput").ap()
    build(nc, *args, out)
    r = run_bass_kernel_spmd(nc, [{f"in_{n}": v for n, v in arrays.items()}], core_ids=[0])
    return r.results[0]["out_0"]
```

```python
import concourse.bass as bass
from concourse import mybir
from contextlib import ExitStack

F32 = mybir.dt.float32
F32R = mybir.dt.float32r
I32 = mybir.dt.int32
ALU = mybir.AluOpType
ACT = mybir.ActivationFunctionType
AX = mybir.AxisListType

P = 128
N = 6250
D = 256
KD = D // P
TILES = -(-N // P)
FULL = N // P
LAST = N - FULL * P
NPAD = TILES * P
EDGES = 206250
EPT = 8
QT = 4
GE = EPT * P
GROUPS = -(-EDGES // GE)
REPEATED = GROUPS * GE - EDGES
COLS = GROUPS * EPT
QUADS = COLS // QT
SUMS = QT
ROWS = TILES * P + P
HEADS, DH = 8, 64
INNER = HEADS * DH
PAIRS = HEADS // 2
EXPERTS = 8
EPS = 1e-5
GB = GROUPS // 2
CH = 250
CHUNKS = N // CH
CT = 7


class Chain:

    def __init__(self, eng, sem, base=0):
        self.eng, self.sem, self.base, self.n = eng, sem, base, 0

    def __call__(self, ins):
        self.n += 1
        ins.then_inc(self.sem, 1)
        self.eng.wait_ge(self.sem, self.base + self.n)


def over_tiles(eng, count, unroll, body):
    rounds = count // unroll
    with eng.Fori(0, rounds) as i:
        for u in range(unroll):
            body(i * unroll + u, u)
    for t in range(rounds * unroll, count):
        body(t, t % unroll)


def build(nc, x, src, dst, ew, src_rows, w_gnn, b_gnn, w_kvT, w_q, w_outT, b_out,
          w_routerT, w12, b1T, b2, out):
    ctx = ExitStack()
    with ctx:
        def sb(name, shape, dt=F32):
            return ctx.enter_context(nc.sbuf_tensor(name, shape, dt))

        def ps(name, shape):
            return ctx.enter_context(nc.psum_tensor(name, shape, F32))

        def sem(name):
            return ctx.enter_context(nc.semaphore(name))

        feat_rows = nc.dram_tensor("feat_rows", (ROWS, D), F32).ap()
        edge_sums = [nc.dram_tensor(f"edge_sums{r}", (ROWS, D), F32).ap() for r in range(SUMS)]

        acc = sb("acc", [P, TILES, D])
        xnT = sb("xnT", [P, KD, NPAD])
        wr = sb("wr", [P, KD, EXPERTS])
        b1_sb = sb("b1_sb", [P, EXPERTS, KD])
        b2_sb = sb("b2_sb", [EXPERTS, D])
        ident = sb("ident", [P, P])
        eps = sb("eps", [P, 1])

        first = ctx.enter_context(ExitStack())

        def early(name, shape, dt=F32):
            return first.enter_context(nc.sbuf_tensor(name, shape, dt))

        stats = early("stats", [P, 2 * CHUNKS, 6])
        ln = early("ln", [P, 6, TILES])
        edge_area = early("edge_area", [P, 3 * COLS + 4 * QT * D])
        src_tab = edge_area[:, 0:COLS]
        dst_tab = edge_area[:, COLS:2 * COLS]
        ew_tab = edge_area[:, 2 * COLS:3 * COLS]
        msg = edge_area[:, 3 * COLS:].rearrange("p (s j d) -> p s j d", s=4, j=QT)
        raw = [edge_area[:, (3 + i) * COLS:(4 + i) * COLS].bitcast(I32) for i in range(2)]
        src_row = early("src_row", [P, 4, QT, P], I32)
        same = early("same", [P, 4, QT, P])
        onehot = early("onehot", [P, 2, QT, P])
        joined = early("joined", [P, 2, QT, P])
        window = early("window", [P, 2, D])
        work = early("work", [P, 2, D])
        earlier = early("earlier", [P, P])
        spare = early("spare", [P, 1])
        unused = early("unused", [P, QT, P], mybir.dt.bfloat16)
        clash = early("clash", [P, 4, 3, QT])
        target = early("target", [P, 4, QT], I32)
        wkv = early("wkv", [P, KD, 2 * INNER])
        wq = early("wq", [P, PAIRS, D])
        woT = early("woT", [P, PAIRS, D])
        wg = joined[:, 0, :, :].rearrange("p j e -> p (j e)").rearrange("p (k d) -> p k d", k=KD)
        iota = early("iota", [P, P])
        ones = early("ones", [P, P])
        zeros = early("zeros", [P, D])
        brow = early("brow", [1, 3, D])
        ring = early("ring", [P, 2, KD, P])
        sq = early("sq", [P, 2, HEADS, DH])
        k_sb = early("k_sb", [P, INNER])
        v_sb = early("v_sb", [P, HEADS, DH])
        hs = early("hs", [P, 3, 2 * HEADS])
        fm = early("fm", [P, KD, 4])
        bounds = early("bounds", [P, 2, GROUPS])
        bcol = early("bcol", [GB, 2, 2])
        bcol_i = early("bcol_i", [GB, 2, 1], I32)
        table = early("table", [1, GROUPS + 1], I32)
        dots_sb = early("dots_sb", [P, PAIRS, P])
        pq_sb = sq[:, :, :, :].rearrange("p a h c -> p (a h c)").rearrange("p (q d) -> p q d", q=PAIRS)
        mix = early("mix", [P, KD, D])

        bank = [ps(f"bank{i}", [P, 512]) for i in range(8)]

        s_x = [sem(f"x_loaded{i}") for i in range(5)]
        s_w = sem("weights_loaded")
        s_dst = sem("dst_loaded")
        s_pad = sem("pad_cleared")
        s_const = sem("constants_made")
        s_zero = sem("sums_cleared")
        LOADS = 10
        s_ch = sem("a_vector_chain")
        s_pch = sem("a_pool_chain")
        s_var = sem("a_variance_ready")
        s_std = sem("a_deviation_ready")
        s_row = sem("a_row_ready")
        s_passed = sem("a_vector_waits_passed")
        s_tabs = sem("a_edge_tables_ready")
        s_turn = sem("a_row_turned")
        s_kept = sem("a_row_kept")
        XC = 12
        with nc.Block() as block:
            @block.sync
            def _(sp):
                for c in range(FULL // XC):
                    sp.dma_start(acc[:, c * XC:(c + 1) * XC, :],
                                 x[c * XC * P:(c + 1) * XC * P, :].rearrange("(t p) d -> p t d", p=P)).then_inc(s_x[c], 16)
                sp.wait_ge(s_pad, 1)
                sp.dma_start(acc[0:LAST, FULL, :], x[FULL * P:N, :]).then_inc(s_x[4], 16)
                sp.dma_start(raw[0], dst).then_inc(s_dst, 16)
                sp.dma_start(raw[1], src).then_inc(s_dst, 16)
                n = 0
                for to, of in ((wkv[:, :, :], w_kvT.rearrange("(k p) e -> p k e", p=P)),
                               (ew_tab, ew),
                               (wg[:, :, :], w_gnn.rearrange("(k p) e -> p k e", p=P)),
                               (wq[:, :, :], w_q.rearrange("(k p) e -> p k e", p=P)),
                               (woT[:, :, :], w_outT.rearrange("(k p) e -> p k e", p=P)),
                               (wr[:, :, :], w_routerT.rearrange("(k p) e -> p k e", p=P)),
                               (b1_sb[:, :, :], b1T),
                               (b2_sb[:, :], b2),
                               (brow[:, 0, :], b_gnn), (brow[:, 1, :], b_out)):
                    sp.dma_start(to, of).then_inc(s_w, 16)
                    n += 16
                assert n == 16 * LOADS
                sp.wait_ge(s_pad, 2)
                for to in edge_sums[:SUMS // 2]:
                    sp.dma_start(to.rearrange("(t p) d -> p t d", p=P),
                                 zeros[:, :].unsqueeze(1).to_broadcast([P, ROWS // P, D])).then_inc(s_zero, 16)
                sp.dma_start(feat_rows[NPAD:ROWS, :], zeros[:, :]).then_inc(s_zero, 16)
                sp.wait_ge(s_w, n)
                sp.wait_ge(s_dst, 32)

            @block.gpsimd
            def _(pool):
                link = Chain(pool, s_pch)
                link(nc.gpsimd.memset(ident[:, :], 0.0))
                nc.gpsimd.affine_select(out=ident[:, :], in_=ident[:, :], compare_op=ALU.not_equal, fill=1.0, base=0,
                                        pattern=[[-1, P]], channel_multiplier=1).then_inc(s_const, 1)
                nc.gpsimd.iota(iota[:, :], pattern=[[1, P]], base=0, channel_multiplier=0,
                               allow_small_or_imprecise_dtypes=True).then_inc(s_const, 1)
                link(nc.gpsimd.memset(earlier[:, :], 1.0))
                nc.gpsimd.affine_select(out=earlier[:, :], in_=earlier[:, :], compare_op=ALU.is_gt, fill=0.0, base=0,
                                        pattern=[[-1, P]], channel_multiplier=1).then_inc(s_const, 1)
                nc.gpsimd.iota(spare[:, :], pattern=[[0, 1]], base=N, channel_multiplier=1,
                               allow_small_or_imprecise_dtypes=True).then_inc(s_const, 1)

                pool.wait_ge(s_dst, 32)
                nc.gpsimd.tensor_copy(src_tab, raw[1])
                nc.gpsimd.tensor_copy(dst_tab, raw[0]).then_inc(s_tabs, 1)

                pool.wait_ge(s_w, 16 * LOADS)
                tail = ew_tab[:, COLS - EPT:COLS]
                nc.gpsimd.affine_select(out=tail, in_=tail, compare_op=ALU.is_ge, fill=0.0, base=-REPEATED,
                                        pattern=[[P, EPT]], channel_multiplier=1).then_inc(s_const, 1)
                heads = wkv[:, :, :].rearrange("p k (h c) -> p (k h) c", c=DH)
                half = sq[:, :, :, :].rearrange("p a h c -> p (a h c)").rearrange("p (g c) -> p g c", c=DH // 2)
                n = DH // 2
                link(nc.gpsimd.tensor_tensor(half, heads[:, :, 0:n], heads[:, :, n:], ALU.add))
                while n > 1:
                    n //= 2
                    link(nc.gpsimd.tensor_tensor(half[:, :, 0:n], half[:, :, 0:n], half[:, :, n:2 * n], ALU.add))
                link(nc.gpsimd.tensor_scalar_mul(half[:, :, 0], half[:, :, 0], 1.0 / DH))
                link(nc.gpsimd.tensor_tensor(heads, heads, half[:, :, 0:1].to_broadcast([P, 4 * HEADS, DH]), ALU.subtract))
                link(nc.gpsimd.tensor_tensor(brow[:, 2, :], brow[:, 0, :], brow[:, 1, :], ALU.add))

            @block.vector
            def _(dve):
                nc.vector.memset(acc[:, FULL, :], 0.0).then_inc(s_pad, 1)
                link = Chain(dve, s_ch)
                nc.vector.memset(eps[:, :], EPS)
                nc.vector.memset(ones[:, :], 1.0)
                nc.vector.memset(zeros[:, :], 0.0).then_inc(s_pad, 1)
                link(nc.vector.memset(dots_sb[:, :, :], 0.0))
                for c in range(FULL // XC):
                    dve.wait_ge(s_x[c], 16)
                    for t in range(c * XC, (c + 1) * XC):
                        nc.vector.bn_stats(stats[:, t % (2 * CHUNKS), :], acc[:, t, :])
                dve.wait_ge(s_x[4], 16)
                link(nc.vector.bn_stats(stats[:, FULL, :], acc[:, FULL, :]))
                row_statistics(link, nc, stats, ln, TILES, s_var)
                dve.wait_ge(s_std, 1)
                link(nc.vector.reciprocal(ln[:, 1, :], ln[:, 2, :]))
                base = link.n

                def row(t, slot):
                    dve.wait_ge(s_turn, t + 1)
                    nc.vector.tensor_scalar(work[:, slot, :], acc[:, bass.ds(t, 1), :], ln[:, 0, bass.ds(t, 1)],
                                            ln[:, 1, bass.ds(t, 1)], ALU.subtract, ALU.mult).then_inc(s_row, 1)

                def chunk(c, kept):
                    dve.wait_ge(s_kept, kept)
                    dve.sem_inc(s_passed, 1)
                    for k in range(KD):
                        last = nc.vector.bn_stats(stats[:, bass.ds(c + k * CHUNKS, 1), :].rearrange("p c s -> p (c s)"),
                                                  xnT[:, k, bass.ds(c * CH, CH)])
                    return last
                row(0, 0)
                row(1, 1)
                with dve.Fori(1, TILES // 2) as i:
                    row(i * 2, 0)
                    row(i * 2 + 1, 1)
                    chunk(i - 1, i * 2 + 2)
                row(TILES - 1, 0)
                for c in range(TILES // 2 - 1, CHUNKS):
                    last = chunk(c, TILES + 2)
                link(last)
                for k in range(KD):
                    link(nc.vector.bn_aggr(fm[:, k, 0:2], stats[:, k * CHUNKS:(k + 1) * CHUNKS, :].rearrange("p c s -> p (c s)")))
                nc.vector.tensor_copy(fm[:, 0, 2:3], fm[:, 0, 1:2]).then_inc(s_var, 1)

                dve.wait_ge(s_tabs, 1)
                by_group = dst_tab.rearrange("p (g j) -> p g j", j=EPT)
                nc.vector.tensor_reduce(bounds[:, 0, :], by_group, AX.X, ALU.min)
                nc.vector.tensor_reduce(bounds[:, 1, :], by_group, AX.X, ALU.max)
                dve.wait_ge(s_std, 3)
                for k in range(KD):
                    link(nc.vector.tensor_scalar_add(fm[:, k, 2:3], fm[:, k, 3:4], 1e-4))
                    link(nc.vector.reciprocal(fm[:, k, 3:4], fm[:, k, 2:3]))

            @block.scalar
            def _(act):
                act.wait_ge(s_var, 1)
                nc.scalar.activation(ln[:, 2, :], ln[:, 1, :], ACT.Sqrt, bias=eps[:, :]).then_inc(s_std, 1)

                def keep(t, slot):
                    act.wait_ge(s_turn, t + 3)
                    to = xnT[:, :, bass.ds(t * P, P)]
                    nc.scalar.copy(to, bank[slot][:, 0:D].rearrange("p (k n) -> p k n", k=KD)).then_inc(s_kept, 1)
                act.sem_inc(s_kept, 2)
                over_tiles(act, TILES, 2, keep)
                act.wait_ge(s_var, 2)
                for k in range(KD):
                    nc.scalar.activation(fm[:, k, 3:4], fm[:, k, 1:2], ACT.Sqrt, scale=N / (N - 1.0)).then_inc(s_std, 1)

            @block.tensor
            def _(pe):
                pe.wait_ge(s_const, 1)
                pe.sem_inc(s_turn, 2)

                def turn(t, slot):
                    pe.wait_ge(s_row, t + 1)
                    pe.wait_ge(s_kept, t + 1)
                    for k in range(KD):
                        last = nc.tensor.transpose(bank[slot][:, k * P:(k + 1) * P], work[:, slot, k * P:(k + 1) * P], ident[:, :])
                    last.then_inc(s_turn, 1)
                over_tiles(pe, TILES, 2, turn)

        b_ready = sem("b_operand_ready")
        b_done = sem("b_product_ready")
        b_copied = sem("b_product_copied")
        FS = 8
        assert TILES % FS == 1
        feat_out = msg[:, 0:FS // QT, :, :].rearrange("p s j d -> p (s j) d")
        b_stored = [sem(f"b_rows_stored{i}") for i in range(FS // 2)]
        b_ch = sem("b_vector_chain")
        b_bt = sem("b_bounds_turned")
        b_bc = sem("b_bounds_columns")
        b_br = sem("b_bounds_rows")
        with nc.Block() as block:
            @block.vector
            def _(dve):
                def operand(t, slot):
                    dve.wait_ge(b_done, t + 1)
                    for k in range(KD):
                        last = nc.vector.tensor_scalar(ring[:, slot, k, :], xnT[:, k, bass.ds(t * P, P)], fm[:, k, 0:1],
                                                       fm[:, k, 3:4], ALU.subtract, ALU.mult)
                    last.then_inc(b_ready, 1)
                over_tiles(dve, TILES, 2, operand)

                link = Chain(dve, b_ch)
                dve.wait_ge(b_bt, 1)
                for b in range(2):
                    for m, op in ((0, ALU.min), (1, ALU.max)):
                        link(nc.vector.tensor_reduce(bcol[:, b, m:m + 1], bank[2 + b][0:GB, m * P:(m + 1) * P], AX.X, op))
                link(nc.vector.tensor_tensor(bcol_i[:, :, :], bcol[:, :, 1:2], bcol[:, :, 0:1], ALU.subtract))
                link(nc.vector.tensor_single_scalar(bcol_i[:, :, :], bcol_i[:, :, :], 7, ALU.arith_shift_right))
                nc.vector.tensor_copy(bcol[:, :, 1:2], bcol_i[:, :, :]).then_inc(b_bc, 1)
                dve.wait_ge(b_br, 1)
                nc.vector.tensor_copy(table[:, 0:GROUPS], bank[4][0:1, 0:GROUPS])
                nc.vector.tensor_reduce(table[:, GROUPS:], bank[4][0:1, 256:256 + GROUPS], AX.X, ALU.max)
                by_group = dst_tab.rearrange("p (g j) -> p g j", j=EPT)
                link(nc.vector.tensor_tensor(by_group, by_group, bank[6][:, 0:GROUPS].unsqueeze(2).to_broadcast([P, GROUPS, EPT]),
                                             ALU.subtract))

            @block.tensor
            def _(pe):
                pe.sem_inc(b_done, 2)

                def product(t, slot):
                    pe.wait_ge(b_ready, t + 1)
                    pe.wait_ge(b_copied, t + 1)
                    for k in range(KD):
                        last = nc.tensor.matmul(bank[slot][:, 0:D], ring[:, slot, k, :], wg[:, k, :], start=k == 0, stop=k == KD - 1)
                    last.then_inc(b_done, 1)
                over_tiles(pe, TILES, 2, product)

                for b in range(2):
                    for m in range(2):
                        last = nc.tensor.transpose(bank[2 + b][0:GB, m * P:(m + 1) * P],
                                                   bounds[:, m, b * GB:(b + 1) * GB], ident[:, :])
                last.then_inc(b_bt, 1)
                pe.wait_ge(b_bc, 1)
                for m in range(2):
                    for b in range(2):
                        nc.tensor.matmul(bank[4][0:1, m * 256 + b * GB:m * 256 + (b + 1) * GB], bcol[:, b, m:m + 1],
                                         ident[0:GB, 0:GB], start=True, stop=True)
                for b in range(2):
                    last = nc.tensor.matmul(bank[6][:, b * GB:(b + 1) * GB], bcol[:, b, 0:1].to_broadcast([GB, P]),
                                            ident[0:GB, 0:GB], start=True, stop=True)
                last.then_inc(b_br, 1)

            @block.scalar
            def _(act):
                act.sem_inc(b_copied, 2)

                for stored in b_stored:
                    act.sem_inc(stored, 16)

                def rows(t, u, turn):
                    act.wait_ge(b_done, t + 3)
                    if u % 2 == 0:
                        act.wait_ge(b_stored[u // 2], turn * 16 + 16)
                    nc.scalar.copy(feat_out[:, u, :], bank[u % 2][:, 0:D]).then_inc(b_copied, 1)
                with act.Fori(0, TILES // FS) as i:
                    for u in range(FS):
                        rows(i * FS + u, u, i)
                rows(TILES - 1, 0, TILES // FS)

            @block.sync
            def _(sp):
                def by_tile(rows, count):
                    return rows.rearrange("(t p) d -> p t d", p=P), zeros[:, :].unsqueeze(1).to_broadcast([P, count, D])

                with sp.Fori(0, TILES // FS) as i:
                    for u in range(0, FS, 2):
                        t = i * FS + u
                        sp.wait_ge(b_copied, t + 4)
                        sp.dma_start(feat_rows[bass.ds(t * P, 2 * P), :].rearrange("(t p) d -> p t d", p=P),
                                     feat_out[:, u:u + 2, :]).then_inc(b_stored[u // 2], 16)
                        for sums in edge_sums[SUMS // 2:]:
                            sp.dma_start(*by_tile(sums[bass.ds(t * P, 2 * P), :], 2)).then_inc(s_zero, 16)
                sp.wait_ge(b_copied, TILES + 2)
                sp.dma_start(feat_rows[(TILES - 1) * P:TILES * P, :], feat_out[:, 0, :]).then_inc(b_stored[0], 16)
                for sums in edge_sums[SUMS // 2:]:
                    sp.dma_start(*by_tile(sums[(TILES - 1) * P:, :], ROWS // P - TILES + 1)).then_inc(s_zero, 16)
                sp.wait_ge(s_zero, 16 * (SUMS // 2 + 1 + SUMS // 2 * (TILES // 2 + 1)))
                for n, stored in enumerate(b_stored):
                    sp.wait_ge(stored, 16 * (TILES // FS + (2 if n == 0 else 1)))

        edge_phase(
            nc, sem, acc=acc, xnT=xnT, src_tab=src_tab, dst_tab=dst_tab, ew_tab=ew_tab, msg=msg, src_row=src_row, same=same,
            onehot=onehot, joined=joined, window=window,
            earlier=earlier, spare=spare, clash=clash, unused=unused, target=target, src_rows=src_rows,
            wkv=wkv, wq=wq, woT=woT, iota=iota, ones=ones, eps=eps, zeros=zeros, brow=brow,
            ring=ring, sq=sq, k_sb=k_sb, v_sb=v_sb, hs=hs, table=table, dots_sb=dots_sb, pq_sb=pq_sb, mix=mix,
            bank=bank, feat_rows=feat_rows, edge_sums=edge_sums)
        first.close()
        expert_phase(nc, sb, sem, edge_sums=edge_sums, acc=acc, yT=xnT, w12=w12, wr=wr, b1_sb=b1_sb, b2_sb=b2_sb,
                     ident=ident, eps=eps, bank=bank, out=out)


def row_statistics(link, nc, stats, ln, rows, signal):
    even, odd = stats[:, 0:rows, 1], stats[:, 0:rows, 4]
    link(nc.vector.tensor_tensor(ln[:, 0, 0:rows], even, odd, ALU.add))
    link(nc.vector.tensor_tensor(ln[:, 3, 0:rows], even, odd, ALU.subtract))
    link(nc.vector.tensor_scalar_mul(ln[:, 0, 0:rows], ln[:, 0, 0:rows], 0.5))
    link(nc.vector.tensor_tensor(ln[:, 4, 0:rows], stats[:, 0:rows, 2], stats[:, 0:rows, 5], ALU.add))
    link(nc.vector.tensor_tensor(ln[:, 3, 0:rows], ln[:, 3, 0:rows], ln[:, 3, 0:rows], ALU.mult))
    link(nc.vector.tensor_scalar_mul(ln[:, 4, 0:rows], ln[:, 4, 0:rows], 1.0 / D))
    nc.vector.scalar_tensor_tensor(out=ln[:, 1, 0:rows], in0=ln[:, 3, 0:rows], scalar=0.25, in1=ln[:, 4, 0:rows], op0=ALU.mult,
                                   op1=ALU.add).then_inc(signal, 1)


def edge_phase(nc, sem, *, acc, xnT, src_tab, dst_tab, ew_tab, msg, src_row, same, onehot, joined, window,
               earlier, spare, clash, unused, target, src_rows, wkv, wq, woT,
               iota, ones, eps, zeros, brow, ring, sq, k_sb, v_sb, hs, table, dots_sb, pq_sb, mix, bank,
               feat_rows, edge_sums):
    jbank, mbank = bank[0], [bank[1], bank[2]]
    kb, vb, dots, mm = bank[3], bank[4], bank[5], bank[6]
    QPI = 4
    ITERS = QUADS // QPI

    rows_in = [sem(f"c_sources_loaded{i}") for i in range(2)]
    win_in = [sem(f"c_window_loaded{i}") for i in range(2)]
    same_made = sem("c_same_made")
    built = sem("c_matrices_built")
    idx_ch = sem("c_index_chain")
    j_done = sem("c_joined_ready")
    j_kept = sem("c_joined_kept")
    m_done = sem("c_messages_ready")
    m_kept = sem("c_messages_kept")
    scattered = [sem(f"c_scattered{r}") for r in range(SUMS)]
    shifted = sem("c_windows_shifted")
    aimed = sem("c_targets_ready")
    ring_ready = sem("c_ring_ready")
    kv_done = sem("c_kv_ready")
    sq_done = sem("c_squares_ready")
    k_kept = sem("c_k_kept")
    ss_done = sem("c_square_sums_ready")
    sd_done = sem("c_deviations_ready")
    c_ch = sem("c_vector_chain")
    v_ready = sem("c_v_ready")
    dots_done = sem("c_dots_added")
    dots_kept = sem("c_dots_kept")
    p_done = sem("c_p_ready")
    p_kept = sem("c_p_kept")
    mix_done = sem("c_mix_ready")
    mix_kept = sem("c_mix_kept")
    mm_done = sem("c_mixed_ready")
    mm_added = sem("c_mixed_added")
    act_waits = sem("c_act_waits_passed")
    sp_waits = sem("c_sync_waits_passed")


    def slot_free(eng, v, u):
        if not isinstance(v, int) or v:
            for j in range(QT):
                eng.wait_ge(scattered[j], (v * QPI + u - (QPI - 1)) * 16)

    def back(v, u):
        return (v, u - 1) if u else (v - 1, QPI - 1)

    def further_passes(eng, one):
        passes = eng.value_load(table[0:1, GROUPS:GROUPS + 1], min_val=0, max_val=TILES)
        with eng.If(0 < passes):
            with eng.Fori(1, passes + 1) as w:
                one(w, w * ITERS)

    with nc.Block() as block:
        @block.sync
        def _(sp):
            def load(v, i, h):
                sp.wait_ge(built, v * QPI + h * 2 + 2)
                sp.sem_inc(sp_waits, 1)
                row = src_rows[bass.ds((i * 2 + h) * GE, GE)].unsqueeze(0).to_broadcast([P, GE])
                sp.dma_start(src_row[:, 2 * h:2 * h + 2, :, :].rearrange("p u j e -> p (u j e)"), row).then_inc(rows_in[h], 16)
                sp.wait_ge(m_done, (v * 2 + h) * 4 + 4)
                sp.sem_inc(sp_waits, 1)
                start = sp.value_load(table[0:1, bass.ds(i * 2 + h, 1)], min_val=0, max_val=N - 1)
                sp.dma_start(window[:, h, :], feat_rows[bass.ds(start, P), :]).then_inc(win_in[h], 16)

            with sp.Fori(0, ITERS) as i:
                load(i, i, 0)
                load(i, i, 1)

            def again(w, v):
                sp.wait_ge(shifted, w)
                sp.sem_inc(sp_waits, 1)
                with sp.Fori(0, ITERS) as i:
                    load(v + i, i, 0)
                    load(v + i, i, 1)
            further_passes(sp, again)

        @block.gpsimd
        def _(pool):
            def scatter(v, u):
                pool.wait_ge(m_kept, (v * QPI + u) * 2 + 4)
                pool.sem_inc(pool_waits, 1)
                pool.wait_ge(aimed, v * QPI + u + 1)
                pool.sem_inc(pool_waits, 1)
                for j in range(QT):
                    if not isinstance(v, int) or u:
                        pool.wait_ge(scattered[j], (v * QPI + u) * 16)
                        pool.sem_inc(pool_waits, 1)
                    nc.gpsimd.indirect_dma_start(
                        out=edge_sums[j], out_offset=bass.IndirectOffsetOnAxis(ap=target[:, u, j:j + 1], axis=0),
                        in_=msg[:, u, j, :], in_offset=None, compute_op=ALU.add).then_inc(scattered[j], 16)
            pool_waits = sem("c_pool_waits_passed")
            for u in range(QPI):
                scatter(0, u)
            with pool.Fori(1, ITERS) as i:
                for u in range(QPI):
                    scatter(i, u)

            def again(w, v):
                with pool.Fori(0, ITERS) as i:
                    for u in range(QPI):
                        scatter(v + i, u)
                for r in range(SUMS):
                    pool.wait_ge(scattered[r], (v + ITERS) * (QPI * 16))
                    pool.sem_inc(pool_waits, 1)
            for r in range(SUMS):
                pool.wait_ge(scattered[r], ITERS * QPI * 16)
                pool.sem_inc(pool_waits, 1)
            further_passes(pool, again)

        @block.tensor
        def _(pe):
            pe.sem_inc(m_done, 8)
            pe.sem_inc(j_done, 2)

            def join(v, u):
                q = v * QPI + u
                pe.wait_ge(built, q + 5)
                pe.wait_ge(j_kept, q + 1)
                for j in range(QT):
                    last = nc.tensor.matmul(jbank[:, j * P:(j + 1) * P], onehot[:, u % 2, j, :], same[:, u, j, :],
                                            start=True, stop=True)
                last.then_inc(j_done, 1)

            def messages(v, u):
                q = v * QPI + u
                pe.wait_ge(win_in[u // 2], v * 16 + 16)
                pe.wait_ge(j_kept, q + 2)
                for b in range(2):
                    pe.wait_ge(m_kept, q * 2 + b + 1)
                    for j in range(2):
                        last = nc.tensor.matmul(mbank[b][:, j * D:(j + 1) * D], joined[:, u % 2, 2 * b + j, :],
                                                window[:, u // 2, :], start=True, stop=True)
                    last.then_inc(m_done, 1)

            def attend(i, u):
                if u == 0:
                    pe.wait_ge(ring_ready, i + 1)
                    pe.wait_ge(k_kept, i + 1)
                if u == 1:
                    if not isinstance(i, int):
                        dot(i - 1)
                    pe.wait_ge(v_ready, i + 1)
                if u <= 1:
                    for k in range(KD):
                        last = nc.tensor.matmul((kb, vb)[u][:, :], ring[:, 0, k, :], wkv[:, k, u * INNER:(u + 1) * INNER],
                                                start=k == 0, stop=k == KD - 1)
                if u == 1:
                    last.then_inc(kv_done, 1)

            def dot(i):
                pe.wait_ge(v_ready, i + 2)
                pe.wait_ge(k_kept, i + 2)
                for q in range(PAIRS):
                    last = nc.tensor.matmul(dots[:, q * P:(q + 1) * P], v_sb[:, 2 * q:2 * q + 2, :].rearrange("p h c -> p (h c)"),
                                            k_sb[:, q * P:(q + 1) * P], start=False, stop=False, skip_group_check=True)
                last.then_inc(dots_done, 1)

            def mixed(i, u):
                if u:
                    return
                pe.wait_ge(ring_ready, i + 1)
                pe.wait_ge(mm_added, i + 1 - TILES)
                for k in range(KD):
                    nc.tensor.matmul(mm[:, 0:D], ring[:, 0, k, :], mix[:, k, :], start=k == 0, stop=False)
                nc.tensor.matmul(mm[:, 0:D], ones[0:1, :], brow[0:1, 2, :], start=False, stop=True).then_inc(mm_done, 1)

            def step(v, first=False, other=None):
                for u in range(QPI):
                    join(v, u)
                    if u or not first:
                        messages(*back(v, u))
                    if other:
                        other(v, u)

            nc.tensor.matmul(dots[:, :], zeros[:, 0:P], wkv[:, 0, 0:512], start=True, stop=False, skip_group_check=True)
            step(0, True, attend)
            with pe.Fori(1, TILES) as i:
                step(i, False, attend)
            dot(TILES - 1)
            nc.tensor.matmul(dots[:, :], zeros[:, 0:P], wkv[:, 0, 0:512], start=False, stop=True,
                             skip_group_check=True).then_inc(dots_done, 1)

            pe.wait_ge(dots_kept, 1)
            for q in range(PAIRS):
                b = (kb, vb)[q % 2]
                if q >= 2:
                    pe.wait_ge(p_kept, q - 1)
                nc.tensor.matmul(b[:, 0:D], dots_sb[:, q, :], woT[:, q, :], start=True, stop=True).then_inc(p_done, 1)
            pe.wait_ge(p_kept, PAIRS)
            for k in range(KD):
                for q in range(PAIRS):
                    last = nc.tensor.matmul(mm[:, k * D:(k + 1) * D], wq[:, q, k * P:(k + 1) * P], pq_sb[:, q, :],
                                            start=q == 0, stop=q == PAIRS - 1)
            last.then_inc(mix_done, 1)
            pe.wait_ge(mix_kept, 1)
            with pe.Fori(TILES, 2 * TILES) as i:
                step(i, False, mixed)
            with pe.Fori(2 * TILES, ITERS) as i:
                step(i)
            messages(ITERS - 1, QPI - 1)

            def again(w, v):
                step(v, True)
                with pe.Fori(1, ITERS) as i:
                    step(v + i)
                messages(v + (ITERS - 1), QPI - 1)
            further_passes(pe, again)

        @block.scalar
        def _(act):
            act.sem_inc(k_kept, 1)
            act.sem_inc(j_kept, 1)
            act.sem_inc(m_kept, 2)

            def keep_joined(v, u):
                q = v * QPI + u
                act.wait_ge(j_done, q + 3)
                nc.scalar.copy(joined[:, u % 2, :, :].rearrange("p j e -> p (j e)"), jbank[:, :]).then_inc(j_kept, 1)

            def rows(v, u):
                q = v * QPI + u
                slot_free(act, v, u)
                for b in range(2):
                    act.wait_ge(m_done, q * 2 + b + 9)
                    nc.scalar.copy(msg[:, u, 2 * b:2 * b + 2, :].rearrange("p j d -> p (j d)"), mbank[b][:, :]).then_inc(m_kept, 1)

            def keys(i):
                act.wait_ge(kv_done, i + 1)
                nc.scalar.activation(sq[:, 0, :, :].rearrange("p h c -> p (h c)"), kb[:, :], ACT.Square)
                nc.scalar.activation(sq[:, 1, :, :].rearrange("p h c -> p (h c)"), vb[:, :], ACT.Square).then_inc(sq_done, 1)
                act.wait_ge(dots_done, i + 1)
                nc.scalar.copy(k_sb[:, :], kb[:, :]).then_inc(k_kept, 1)

            def deviations(i):
                act.wait_ge(ss_done, i + 1)
                nc.scalar.activation(hs[:, 1, :], hs[:, 0, :], ACT.Sqrt, bias=eps[:, :], scale=1.0 / DH).then_inc(sd_done, 1)

            def operand(t):
                nc.scalar.copy(ring[:, 0, :, :], xnT[:, :, bass.ds(t * P, P)]).then_inc(ring_ready, 1)

            def attention(i, u):
                if u == 1:
                    keys(i)
                    operand(i + 1)
                if u == 3:
                    deviations(i)

            def mixing(i, u):
                if u == 0:
                    act.wait_ge(mm_done, i + 1 - TILES)
                    act.sem_inc(act_waits, 1)
                    operand(i + 1 - TILES)

            def step(v, first=False, other=None):
                for u in range(QPI):
                    keep_joined(v, u)
                    if u or not first:
                        rows(*back(v, u))
                    if other:
                        other(v, u)

            def last_attention(i, u):
                if u == 1:
                    keys(i)
                if u == 3:
                    deviations(i)

            operand(0)
            step(0, True, attention)
            with act.Fori(1, TILES - 1) as i:
                step(i, False, attention)
            step(TILES - 1, False, last_attention)
            for q in range(PAIRS):
                act.wait_ge(p_done, q + 1)
                nc.scalar.copy(pq_sb[:, q, :], (kb, vb)[q % 2][:, 0:D]).then_inc(p_kept, 1)
            act.wait_ge(mix_done, 1)
            nc.scalar.copy(mix[:, :, :], mm[:, :].rearrange("p (k d) -> p k d", k=KD)).then_inc(mix_kept, 1)
            operand(0)
            with act.Fori(TILES, 2 * TILES - 1) as i:
                step(i, False, mixing)
            with act.Fori(2 * TILES - 1, ITERS) as i:
                step(i)
            rows(ITERS - 1, QPI - 1)

            def again(w, v):
                step(v, True)
                with act.Fori(1, ITERS) as i:
                    step(v + i)
                rows(v + (ITERS - 1), QPI - 1)
            further_passes(act, again)

        @block.vector
        def _(dve):
            dve.sem_inc(built, 4)
            dve.sem_inc(v_ready, 1)
            dve.sem_inc(dots_done, 1)
            dve.sem_inc(mm_added, 1)

            def build(v, i, u):
                q = v * QPI + u
                at = i * (QPI * QT) + u * QT
                if u % 2 == 0:
                    dve.wait_ge(rows_in[u // 2], v * 16 + 16)
                for j in range(QT):
                    last = nc.vector.tensor_scalar(same[:, u, j, :], src_row[:, u, j, :],
                                                   src_tab[:, bass.ds(at + j, 1)], None, ALU.is_equal)
                last.then_inc(same_made, 1)
                dve.wait_ge(j_done, q + 1)
                for j in range(QT):
                    last = nc.vector.tensor_scalar(onehot[:, u % 2, j, :], iota[:, :], dst_tab[:, bass.ds(at + j, 1)],
                                                   ew_tab[:, bass.ds(at + j, 1)], ALU.is_equal, ALU.mult)
                last.then_inc(built, 1)

            def targets(v, i, u):
                q = v * QPI + u
                dve.wait_ge(same_made, q + 1)
                slot_free(dve, v, u)
                link = Chain(dve, idx_ch, q * 3)
                clashes, hit, off = (clash[:, u, n, :] for n in range(3))
                for j in range(QT):
                    last = nc.vector.tensor_tensor_reduce(out=unused[:, j, :], in0=same[:, u, j, :], in1=earlier[:, :],
                                                          scale=1.0, scalar=0.0, op0=ALU.mult, op1=ALU.add,
                                                          accum_out=clashes[:, j:j + 1])
                link(last)
                link(nc.vector.tensor_scalar_min(hit, clashes, 1.0))
                sources = src_tab[:, bass.ds(i * (QPI * QT) + u * QT, QT)]
                link(nc.vector.scalar_tensor_tensor(out=off, in0=sources, scalar=spare[:, :], in1=hit,
                                                    op0=ALU.subtract, op1=ALU.mult))
                nc.vector.tensor_tensor(target[:, u, :], sources, off, ALU.subtract).then_inc(aimed, 1)

            def squares(i):
                dve.wait_ge(sq_done, i + 1)
                nc.vector.tensor_reduce(hs[:, 0, :], sq[:, :, :, :].rearrange("p a h c -> p (a h) c"), AX.X,
                                        ALU.add).then_inc(ss_done, 1)

            def values(i):
                link = Chain(dve, c_ch, i * 2)
                dve.wait_ge(sd_done, i + 1)
                link(nc.vector.reciprocal(hs[:, 2, :], hs[:, 1, :]))
                link(nc.vector.tensor_tensor(hs[:, 2, 0:HEADS], hs[:, 2, 0:HEADS], hs[:, 2, HEADS:], ALU.mult))
                dve.wait_ge(dots_done, i + 1)
                nc.vector.tensor_tensor(v_sb[:, :, :], vb[:, :].rearrange("p (h c) -> p h c", h=HEADS),
                                        hs[:, 2, 0:HEADS].unsqueeze(2).to_broadcast([P, HEADS, DH]), ALU.mult).then_inc(v_ready, 1)

            def attention(i, u):
                if u == 0 and not isinstance(i, int):
                    values(i - 1)
                if u == 3:
                    squares(i)

            def mixed(i, u):
                if u == 2:
                    dve.wait_ge(mm_done, i + 1 - TILES)
                    to = acc[:, bass.ds(i - TILES, 1), :].rearrange("p t d -> p (t d)")
                    nc.vector.tensor_tensor(to, to, mm[:, 0:D], ALU.add).then_inc(mm_added, 1)

            def step(v, i, first=False, other=None):
                for u in range(QPI):
                    build(v, i, u)
                    if u or not first:
                        targets(*back(v, u)[:1], *back(i, u))
                    if other:
                        other(v, u)

            step(0, 0, True, attention)
            with dve.Fori(1, TILES) as i:
                step(i, i, False, attention)
            values(TILES - 1)
            dve.wait_ge(dots_done, TILES + 2)
            for h in range(2):
                blk = dots_sb[h * DH:(h + 1) * DH, :, h * DH:(h + 1) * DH]
                last = nc.vector.tensor_scalar_mul(blk, dots[h * DH:(h + 1) * DH, :].rearrange("p (q d) -> p q d", q=PAIRS)[
                    :, :, h * DH:(h + 1) * DH], 1.0 / N)
            last.then_inc(dots_kept, 1)
            with dve.Fori(TILES, 2 * TILES) as i:
                step(i, i, False, mixed)
            with dve.Fori(2 * TILES, ITERS) as i:
                step(i, i)
            targets(ITERS - 1, ITERS - 1, QPI - 1)

            def again(w, v):
                dve.wait_ge(built, v * QPI + 4)
                for h in range(2):
                    dve.wait_ge(win_in[h], v * 16)
                nc.vector.tensor_scalar_add(dst_tab, dst_tab, -float(P))
                nc.vector.tensor_scalar(table[:, 0:GROUPS], table[:, 0:GROUPS], float(P), N - 1.0, ALU.add, ALU.min
                                        ).then_inc(shifted, 1)
                dve.wait_ge(shifted, w)
                step(v, 0, True)
                with dve.Fori(1, ITERS) as i:
                    step(v + i, i)
                targets(v + (ITERS - 1), ITERS - 1, QPI - 1)
            further_passes(dve, again)


def expert_phase(nc, sb, sem, *, edge_sums, acc, yT, w12, wr, b1_sb, b2_sb, ident, eps, bank, out):
    w_high = sb("w_high", [P, 2, EXPERTS, KD, D], F32R)
    w_low = sb("w_low", [P, 2, EXPERTS, KD, D], F32R)
    router = sb("router", [P, 5, TILES, EXPERTS])
    route1 = sb("route1", [P, 4, TILES])
    rank = sb("rank", [P, EXPERTS])
    combT = sb("combT", [EXPERTS, 2, P])
    comb1 = sb("comb1", [P, 2, EXPERTS])

    with ExitStack() as routing:
        def temp(name, shape):
            return routing.enter_context(nc.sbuf_tensor(name, shape, F32))
        stats = temp("chunk_stats", [P, CT, 6])
        ln = temp("chunk_ln", [P, 6, CT])
        raw_w = temp("raw_w", [P, 2, KD * D])
        y_row = temp("y_row", [P, 2, D])
        ring = temp("y_ring", [P, 2, KD, P])
        route(nc, sem, edge_sums=edge_sums, acc=acc, yT=yT, w12=w12, w_high=w_high, w_low=w_low, raw_w=raw_w,
              y_row=y_row, ring=ring, wr=wr, ident=ident, eps=eps, stats=stats, ln=ln, router=router,
              route1=route1, rank=rank, bank=bank)

    hidden = sb("hidden", [P, 2, KD, 2 * P])
    h_high = sb("h_high", [P, 2, KD, 2 * P], F32R)
    h_low = sb("h_low", [P, 2, KD, 2 * P], F32R)
    y_high = sb("y_high", [P, 2, KD, 2 * P], F32R)
    y_low = sb("y_low", [P, 2, KD, 2 * P], F32R)

    PARTS = ((1, 0), (0, 1), (0, 0))
    PAIR_COUNT = -(-TILES // 2)
    c_staged = sem("f_weights_staged")
    c_turned = sem("f_weights_turned")
    c_kept = sem("f_weights_kept")
    y_high_made = sem("f_operand_high_part_ready")
    y_made = sem("f_operand_ready")
    l1_done = sem("f_hidden_ready")
    gelued = sem("f_gelu_ready")
    h_high_made = sem("f_gelu_high_part_ready")
    h_made = sem("f_gelu_parts_ready")
    l2_done = sem("f_output_ready")
    added = sem("f_output_added")
    b_done = sem("f_bias_ready")
    bias_added = sem("f_bias_added")
    stored = sem("f_stored")
    hp = [bank[0], bank[1]]
    op = [bank[2], bank[3]]
    ctb, bb = bank[4], bank[5]

    h_parts, y_parts, w_parts = (h_high, h_low), (y_high, y_low), (w_high, w_low)

    def over_pairs(eng, pair):
        full = TILES // 2
        rounds = (full - 1) // 2
        with eng.Fori(0, rounds) as i:
            for u in range(2):
                pair(i * 2 + u, u, 2, 2)
        for p in range(rounds * 2, PAIR_COUNT):
            pair(p, p % 2, 2 if p < full else 1, 2 if p + 1 < full else 1 if p + 1 < PAIR_COUNT else 0)

    with nc.Block() as block:
        @block.tensor
        def _(pe):
            def layer1(p, slot, tiles, e):
                n = p * EXPERTS + e
                if e == 0:
                    pe.wait_ge(y_made, p + 1)
                pe.wait_ge(gelued, n + 1)
                for h in range(KD):
                    products = [(a, b, k) for a, b in PARTS for k in range(KD)]
                    for m, (a, b, k) in enumerate(products):
                        last = nc.tensor.matmul(hp[e % 2][:, h * D:h * D + tiles * P], w_parts[a][:, 0, e, k, h * P:(h + 1) * P],
                                                y_parts[b][:, slot, k, 0:tiles * P], start=m == 0, stop=m == len(products) - 1)
                last.then_inc(l1_done, 1)

            def layer2(p, tiles, e):
                n = p * EXPERTS + e
                pe.wait_ge(h_made, n + 3)
                pe.wait_ge(added, n + 1)
                for t in range(tiles):
                    products = [(a, b, k) for a, b in PARTS for k in range(KD)]
                    for m, (a, b, k) in enumerate(products):
                        last = nc.tensor.matmul(op[e % 2][:, t * D:(t + 1) * D], h_parts[a][:, e % 2, k, t * P:(t + 1) * P],
                                                w_parts[b][:, 1, e, k, :], start=m == 0, stop=m == len(products) - 1)
                last.then_inc(l2_done, 1)

            def pair(p, slot, tiles, after):
                pe.wait_ge(c_staged, p + 1)
                for t in range(tiles):
                    last = nc.tensor.transpose(ctb[0:EXPERTS, t * P:(t + 1) * P], comb1[:, t, :], ident[:, :])
                last.then_inc(c_turned, 1)
                for e in range(EXPERTS):
                    if e + 1 < EXPERTS:
                        layer1(p, slot, tiles, e + 1)
                    elif after:
                        layer1(p + 1, 1 - slot, after, 0)
                    if e == 2:
                        pe.wait_ge(c_kept, p + 1)
                        for t in range(tiles):
                            last = nc.tensor.matmul(bb[:, t * D:(t + 1) * D], combT[:, t, :], b2_sb[:, :], start=True, stop=True)
                        last.then_inc(b_done, 1)
                    layer2(p, tiles, e)
            layer1(0, 0, 2, 0)
            over_pairs(pe, pair)

        @block.scalar
        def _(act):
            act.sem_inc(gelued, 2)

            def pair(p, slot, tiles, after):
                for e in range(EXPERTS):
                    n = p * EXPERTS + e
                    act.wait_ge(l1_done, n + 1)
                    act.wait_ge(h_made, n + 1)
                    for h in range(KD):
                        last = nc.scalar.activation(hidden[:, e % 2, h, 0:tiles * P], hp[e % 2][:, h * D:h * D + tiles * P],
                                                    ACT.Gelu, bias=b1_sb[:, e, h:h + 1])
                    last.then_inc(gelued, 1)
            over_pairs(act, pair)

        @block.vector
        def _(dve):
            dve.sem_inc(added, 2)
            dve.sem_inc(h_made, 2)
            dve.sem_inc(l2_done, 2)

            def operand_high(p, slot, tiles):
                nc.vector.tensor_copy(y_high[:, slot, :, 0:tiles * P], yT[:, :, bass.ds(p * 2 * P, tiles * P)]
                                      ).then_inc(y_high_made, 1)

            def operand_low(p, slot, tiles):
                dve.wait_ge(y_high_made, p + 1)
                nc.vector.tensor_tensor(y_low[:, slot, :, 0:tiles * P], yT[:, :, bass.ds(p * 2 * P, tiles * P)],
                                        y_high[:, slot, :, 0:tiles * P].bitcast(F32), ALU.subtract).then_inc(y_made, 1)

            def stage(p, tiles):
                nc.vector.tensor_copy(comb1[:, 0:tiles, :], router[:, 4, bass.ds(p * 2, tiles), :]).then_inc(c_staged, 1)

            def split(p, tiles, e):
                n = p * EXPERTS + e
                high, low = (part[:, e % 2, :, 0:tiles * P] for part in h_parts)
                of = hidden[:, e % 2, :, 0:tiles * P]
                dve.wait_ge(gelued, n + 3)
                dve.wait_ge(l2_done, n + 1)
                nc.vector.tensor_copy(high, of).then_inc(h_high_made, 1)
                dve.wait_ge(h_high_made, n + 1)
                nc.vector.tensor_tensor(low, of, high.bitcast(F32), ALU.subtract).then_inc(h_made, 1)

            def pair(p, slot, tiles, after):
                for e in range(EXPERTS):
                    n = p * EXPERTS + e
                    if e + 1 < EXPERTS:
                        split(p, tiles, e + 1)
                    elif after:
                        split(p + 1, after, 0)
                    if e == 0:
                        dve.wait_ge(c_turned, p + 1)
                        nc.vector.tensor_copy(combT[:, 0:tiles, :], ctb[0:EXPERTS, 0:tiles * P].rearrange("e (t n) -> e t n", t=tiles)
                                              ).then_inc(c_kept, 1)
                    dve.wait_ge(l2_done, n + 3)
                    dve.wait_ge(added, n + 2)
                    for t in range(tiles):
                        to = acc[:, bass.ds(p * 2 + t, 1), :].rearrange("p t d -> p (t d)")
                        last = nc.vector.scalar_tensor_tensor(
                            out=to, in0=op[e % 2][:, t * D:(t + 1) * D],
                            scalar=router[:, 4, bass.ds(p * 2 + t, 1), e:e + 1].rearrange("p t e -> p (t e)"),
                            in1=to, op0=ALU.mult, op1=ALU.add)
                    last.then_inc(added, 1)
                    if e == 3:
                        dve.wait_ge(b_done, p + 1)
                        dve.wait_ge(added, n + 3)
                        to = acc[:, bass.ds(p * 2, tiles), :]
                        nc.vector.tensor_tensor(to, to, bb[:, 0:tiles * D].rearrange("p (t d) -> p t d", t=tiles), ALU.add
                                                ).then_inc(bias_added, 1)
                        dve.wait_ge(bias_added, p + 1)
                    if after and e == 4:
                        dve.wait_ge(l1_done, p * EXPERTS + 1)
                        operand_high(p + 1, 1 - slot, after)
                    if after and e == 5:
                        operand_low(p + 1, 1 - slot, after)
                    if after and e == 6:
                        stage(p + 1, after)
            stage(0, 2)
            operand_high(0, 0, 2)
            operand_low(0, 0, 2)
            split(0, 2, 0)
            over_pairs(dve, pair)

        @block.sync
        def _(sp):
            with sp.Fori(0, FULL // 2) as p:
                sp.wait_ge(added, p * EXPERTS + EXPERTS + 2)
                sp.dma_start(out[bass.ds(p * 2 * P, 2 * P), :].rearrange("(t p) d -> p t d", p=P), acc[:, bass.ds(p * 2, 2), :]
                             ).then_inc(stored, 16)
            sp.wait_ge(added, PAIR_COUNT * EXPERTS + 2)
            sp.dma_start(out[FULL * P:N, :], acc[0:LAST, FULL, :]).then_inc(stored, 16)
            sp.wait_ge(stored, 16 * PAIR_COUNT)


def route(nc, sem, *, edge_sums, acc, yT, w12, w_high, w_low, raw_w, y_row, ring, wr, ident, eps, stats, ln,
          router, route1, rank, bank):
    added = [sem(f"e_sum_added{i}") for i in range(2)]
    w_in = [sem(f"e_expert_weights_loaded{i}") for i in range(2)]
    act_waits = sem("e_act_waits_passed")
    summed = sem("e_vector_waits_passed")
    pool_waits = sem("e_pool_waits_passed")
    row_added = sem("e_row_added")
    ch = sem("e_vector_chain")
    var = sem("e_variance_ready")
    std = sem("e_deviation_ready")
    row = sem("e_row_ready")
    turned = sem("e_row_turned")
    kept = sem("e_row_kept")
    ringed = sem("e_operand_ready")
    logit = sem("e_logits_ready")
    logit_kept = sem("e_logits_kept")
    shifted = sem("e_logits_shifted")
    exped = sem("e_exponentials_ready")
    probs, one1, one2, tmp, comb = (router[:, i, :, :] for i in range(5))
    top, top2, den, inv = (route1[:, i, :] for i in range(4))

    def wide(a):
        return a.unsqueeze(2).to_broadcast([P, TILES, EXPERTS])

    rounded = sem("e_expert_weights_rounded")
    w_split = sem("e_expert_weights_split")
    ranked = sem("e_ranks_made")

    with nc.Block() as block:
        @block.sync
        def _(sp):
            def load(n, slot):
                sp.wait_ge(w_split, n + 1)
                sp.dma_start(raw_w[:, slot, :].rearrange("p (o k n) -> p o k n", o=1, k=KD),
                             w12[bass.ds(n, 1), :, :].rearrange("o (k p) n -> p o k n", p=P)).then_inc(w_in[slot], 16)
            over_tiles(sp, 2 * EXPERTS, 2, load)

        @block.gpsimd
        def _(pool):
            nc.gpsimd.iota(rank[:, :], pattern=[[-1, EXPERTS]], base=EXPERTS, channel_multiplier=0,
                           allow_small_or_imprecise_dtypes=True).then_inc(ranked, 1)

            def add(c, half, turn, r):
                if r or not isinstance(turn, int) or turn:
                    pool.wait_ge(added[half], (turn * SUMS + r) * 16)
                    pool.sem_inc(pool_waits, 1)
                nc.gpsimd.dma_start(acc[:, bass.ds(c * CT, CT), :],
                                    edge_sums[r][bass.ds(c * (CT * P), CT * P), :].rearrange("(t p) d -> p t d", p=P),
                                    accum_op=ALU.add).then_inc(added[half], 16)
            def two(i):
                for r in range(SUMS):
                    for half in range(2):
                        add(i * 2 + half, half, i, r)
            two(0)
            with pool.Fori(1, TILES // CT // 2) as i:
                two(i)
            for r in range(SUMS):
                add(TILES // CT - 1, 0, TILES // CT // 2, r)

        high, low = (w[:, :, :, :, :].rearrange("p l e k n -> p (l e) (k n)") for w in (w_high, w_low))

        def part(of, n):
            return of[:, bass.ds(n, 1), :].rearrange("p o n -> p (o n)")

        def before(t, j):
            return t + 1 if j else t + 2

        @block.vector
        def _(dve):
            dve.sem_inc(w_split, 2)
            dve.sem_inc(logit_kept, 2)
            dve.sem_inc(row_added, 2)
            LINKS = 8

            def low_part(n, slot):
                dve.wait_ge(rounded, n + 1)
                nc.vector.tensor_tensor(part(low, n), raw_w[:, slot, :], part(high, n).bitcast(F32), ALU.subtract).then_inc(w_split, 1)

            def chunk(c, half, turn):
                link = Chain(dve, ch, c * LINKS)
                dve.wait_ge(added[half], (turn + 1) * (SUMS * 16))
                dve.sem_inc(summed, 1)
                for j in range(CT):
                    last = nc.vector.bn_stats(stats[:, j, :], acc[:, bass.ds(c * CT + j, 1), :].rearrange("p t d -> p (t d)"))
                link(last)
                row_statistics(link, nc, stats, ln, CT, var)
                for slot in range(2):
                    low_part(c * 2 + slot, slot)
                dve.wait_ge(std, c + 1)
                link(nc.vector.reciprocal(ln[:, 1, 0:CT], ln[:, 2, 0:CT]))
                assert link.n == LINKS

                def normalise(j):
                    t, slot = c * CT + j, j % 2
                    dve.wait_ge(turned, before(t, j))
                    dve.wait_ge(row_added, before(t, j))
                    nc.vector.tensor_scalar(y_row[:, slot, :], acc[:, bass.ds(t, 1), :].rearrange("p t d -> p (t d)"),
                                            ln[:, 0, j:j + 1], ln[:, 1, j:j + 1], ALU.subtract, ALU.mult).then_inc(row, 1)

                def add(j):
                    t = c * CT + j
                    dve.wait_ge(row, t + 1)
                    to = acc[:, bass.ds(t, 1), :].rearrange("p t d -> p (t d)")
                    nc.vector.tensor_tensor(to, to, y_row[:, j % 2, :], ALU.add).then_inc(row_added, 1)

                def logits(j):
                    t = c * CT + j
                    dve.wait_ge(logit, t + 3)
                    nc.vector.tensor_copy(router[:, 0, bass.ds(t, 1), :].rearrange("p t e -> p (t e)"),
                                          bank[2 + j % 2][:, 0:EXPERTS]).then_inc(logit_kept, 1)
                for j in range(CT + 2):
                    if j < CT:
                        normalise(j)
                    if 1 <= j <= CT:
                        add(j - 1)
                    if j >= 2:
                        logits(j - 2)
            with dve.Fori(0, TILES // CT // 2) as i:
                for half in range(2):
                    chunk(i * 2 + half, half, i)
            chunk(TILES // CT - 1, 0, TILES // CT // 2)
            for n in range(2 * (TILES // CT), 2 * EXPERTS):
                low_part(n, n % 2)
            link = Chain(dve, ch, TILES // CT * LINKS)

            dve.wait_ge(logit_kept, TILES + 2)
            link(nc.vector.tensor_reduce(top, probs, AX.X, ALU.max))
            nc.vector.tensor_tensor(tmp, probs, wide(top), ALU.subtract).then_inc(shifted, 1)
            dve.wait_ge(exped, 1)
            link(nc.vector.tensor_reduce(den, comb, AX.X, ALU.add))
            link(nc.vector.reciprocal(inv, den))
            link(nc.vector.tensor_tensor(probs, comb, wide(inv), ALU.mult))
            dve.wait_ge(ranked, 1)
            by_rank = rank[:, :].unsqueeze(1).to_broadcast([P, TILES, EXPERTS])
            for n, (best, one) in enumerate(((top, one1), (top2, one2))):
                of = probs if n == 0 else comb
                link(nc.vector.tensor_reduce(best, of, AX.X, ALU.max))
                link(nc.vector.tensor_tensor(tmp, of, wide(best), ALU.is_equal))
                link(nc.vector.tensor_tensor(tmp, tmp, by_rank, ALU.mult))
                link(nc.vector.tensor_reduce(den, tmp, AX.X, ALU.max))
                link(nc.vector.tensor_tensor(one, tmp, wide(den), ALU.is_equal))
                if n == 0:
                    link(nc.vector.scalar_tensor_tensor(out=comb, in0=one, scalar=-2.0, in1=probs, op0=ALU.mult, op1=ALU.add))
            link(nc.vector.tensor_tensor(den, top, top2, ALU.add))
            link(nc.vector.tensor_scalar_max(den, den, 1e-12))
            link(nc.vector.reciprocal(inv, den))
            link(nc.vector.tensor_tensor(tmp, one1, one2, ALU.add))
            link(nc.vector.tensor_tensor(tmp, tmp, probs, ALU.mult))
            link(nc.vector.tensor_tensor(comb, tmp, wide(inv), ALU.mult))

        @block.tensor
        def _(pe):
            pe.sem_inc(turned, 2)
            pe.sem_inc(logit, 2)

            with pe.Fori(0, TILES // CT) as c:
                for j in range(CT + 1):
                    if j < CT:
                        t, slot = c * CT + j, j % 2
                        pe.wait_ge(row, t + 1)
                        pe.wait_ge(kept, before(t, j))
                        for k in range(KD):
                            last = nc.tensor.transpose(bank[slot][:, k * P:(k + 1) * P], y_row[:, slot, k * P:(k + 1) * P], ident[:, :])
                        last.then_inc(turned, 1)
                    if j:
                        t, slot = c * CT + j - 1, (j - 1) % 2
                        pe.wait_ge(ringed, t + 1)
                        pe.wait_ge(logit_kept, before(t, j - 1))
                        for k in range(KD):
                            last = nc.tensor.matmul(bank[2 + slot][:, 0:EXPERTS], ring[:, slot, k, :], wr[:, k, :],
                                                    start=k == 0, stop=k == KD - 1)
                        last.then_inc(logit, 1)

        @block.scalar
        def _(act):
            act.sem_inc(kept, 2)

            def high_part(n, slot, turn):
                act.wait_ge(w_in[slot], turn * 16 + 16)
                act.sem_inc(act_waits, 1)
                nc.scalar.copy(part(high, n), raw_w[:, slot, :]).then_inc(rounded, 1)
            with act.Fori(0, TILES // CT) as c:
                for slot in range(2):
                    high_part(c * 2 + slot, slot, c)
                act.wait_ge(var, c + 1)
                nc.scalar.activation(ln[:, 2, 0:CT], ln[:, 1, 0:CT], ACT.Sqrt, bias=eps[:, :]).then_inc(std, 1)
                for j in range(CT):
                    t, slot = c * CT + j, j % 2
                    turned_tile = bank[slot][:, 0:D].rearrange("p (k n) -> p k n", k=KD)
                    act.wait_ge(logit, before(t, j))
                    act.wait_ge(turned, t + 3)
                    nc.scalar.copy(ring[:, slot, :, :], turned_tile).then_inc(ringed, 1)
                    nc.scalar.copy(yT[:, :, bass.ds(t * P, P)], turned_tile).then_inc(kept, 1)
            for n in range(2 * (TILES // CT), 2 * EXPERTS):
                high_part(n, n % 2, n // 2)
            act.wait_ge(shifted, 1)
            nc.scalar.activation(comb, tmp, ACT.Exp).then_inc(exped, 1)


def kernel(**inputs):
    import numpy as np
    import concourse.bacc as bacc
    from concourse.bass_utils import run_bass_kernel_spmd

    def a(name):
        return np.ascontiguousarray(inputs[name])

    def grouped(v):
        return np.concatenate([v[:(GROUPS - 1) * GE], v[EDGES - GE:]])

    def by_partition(v):
        return np.ascontiguousarray(grouped(v).reshape(COLS, P).T)

    qkv = a("L0_mix_w_qkv")
    arrays = {
        "x": a("x"), "src": by_partition(a("src")), "dst": by_partition(a("dst")), "ew": by_partition(a("edge_weight")),
        "src_rows": grouped(a("src")),
        "w_gnn": a("L0_gnn_weight"), "b_gnn": a("L0_gnn_bias").reshape(1, D),
        "w_kvT": np.ascontiguousarray(qkv[INNER:].T), "w_q": np.ascontiguousarray(qkv[:INNER]),
        "w_outT": np.ascontiguousarray(a("L0_mix_w_out").T), "b_out": a("L0_mix_b_out").reshape(1, D),
        "w_routerT": np.ascontiguousarray(a("L0_ffn_router_w").T), "w12": np.concatenate([a("L0_ffn_w1"), a("L0_ffn_w2")]),
        "b1T": np.ascontiguousarray(a("L0_ffn_b1").reshape(EXPERTS, KD, P).transpose(2, 0, 1)), "b2": a("L0_ffn_b2"),
    }
    nc = bacc.Bacc("TRN2", target_bir_lowering=False, num_devices=1)
    args = [nc.dram_tensor(f"in_{n}", v.shape, mybir.dt.from_np(v.dtype), kind="ExternalInput").ap() for n, v in arrays.items()]
    out = nc.dram_tensor("out_0", (N, D), F32, kind="ExternalOutput").ap()
    build(nc, *args, out)
    r = run_bass_kernel_spmd(nc, [{f"in_{n}": v for n, v in arrays.items()}], core_ids=[0])
    return r.results[0]["out_0"]
```
